# Optimizing a Trainium2 kernel written in Bass

```python
import numpy as np
import jax
import jax.numpy as jnp

def _softmax(x, axis=-1):
    return jax.nn.softmax(x, axis=axis)

def _gelu(x):
    return jax.nn.gelu(x, approximate=True)

def _silu(x):
    return jax.nn.silu(x)

def _sigmoid(x):
    return jax.nn.sigmoid(x)

def _layernorm(x, axis=-1, eps=1e-05):
    m = jnp.mean(x, axis=axis, keepdims=True)
    v = jnp.var(x, axis=axis, keepdims=True)
    return (x - m) / jnp.sqrt(v + eps)

def _scatter_add(tgt, idx, src, axis=0):
    return tgt.at[idx].add(src)

def _segment_sum(src, seg, n):
    return jax.ops.segment_sum(src, seg, n)
kernel_name = 'mk_flamingo_gated_d2_seqx_r8_2c9d9b'

def setup_inputs(seed: int=0):
    np.random.seed(seed)
    _w = jnp.asarray

    def _rec_inputs():
        import jax
        import jax.numpy as jnp
        _rk = jax.random.key(seed)
        x = -0.0003929 + 0.9999 * jax.random.normal(jax.random.fold_in(_rk, 1), (2, 512, 128), jnp.float32)
        _lenS = 512 - jax.random.randint(jax.random.fold_in(_rk, 7), (2,), 0, max(1, 512 // 4) + 1, jnp.int32)
        _lenS2 = 32 - jax.random.randint(jax.random.fold_in(_rk, 8), (2,), 0, max(1, 32 // 4) + 1, jnp.int32)
        _ctx_768P = jax.random.normal(jax.random.fold_in(_rk, 11), (2, 16, 96), jnp.float32)
        _ctx_768c = jax.random.dirichlet(jax.random.fold_in(_rk, 511), 0.3 * jnp.ones((16,), jnp.float32), (2, 32))
        _ctx_768t = jnp.einsum('bsk,bkd->bsd', _ctx_768c, _ctx_768P)
        _ctx_768t = _ctx_768t * jax.lax.rsqrt(jnp.mean(jnp.square(_ctx_768t)) + 1e-12) * 0.953939
        ctx_768 = -7.36909e-05 + 0.999899 * (_ctx_768t + 0.3 * jax.random.normal(jax.random.fold_in(_rk, 611), (2, 32, 96), jnp.float32))
        _g = jax.random.normal(jax.random.fold_in(_rk, 9001), (2, 2), jnp.float32)
        _g = jnp.sign(_g) * jnp.maximum(jnp.abs(_g), 1.0) + (_g == 0) * 1.0
        g_xattn = _g[0]
        g_ffn = _g[1]
        return (x, ctx_768, g_xattn, g_ffn)
    x, ctx_768, g_xattn, g_ffn = _rec_inputs()

    def _L0_xattn_setup():
        import jax, jax.numpy as jnp
        import numpy as np
        EPS = 1e-05

        def layernorm(x, g, b):
            mu = jnp.mean(x, axis=-1, keepdims=True)
            var = jnp.mean(jnp.square(x - mu), axis=-1, keepdims=True)
            return (x - mu) * jax.lax.rsqrt(var + EPS) * g + b
        key = jax.random.key(seed)
        ks = jax.random.split(key, 12)
        B, L1, L2 = (8, 256, 256)
        D1, D2, E = (128, 96, 128)
        s1, s2, se = (D1 ** (-0.5), D2 ** (-0.5), E ** (-0.5))
        return {'modality1': jax.random.normal(ks[0], (B, L1, D1), jnp.float32), 'modality2': jax.random.normal(ks[1], (B, L2, D2), jnp.float32), 'ln1_g': jnp.ones((D1,), jnp.float32), 'ln1_b': jnp.zeros((D1,), jnp.float32), 'ln2_g': jnp.ones((D2,), jnp.float32), 'ln2_b': jnp.zeros((D2,), jnp.float32), 'Wq': jax.random.normal(ks[2], (D1, E), jnp.float32) * s1, 'bq': jax.random.normal(ks[3], (E,), jnp.float32) * 0.01, 'Wk': jax.random.normal(ks[4], (D2, E), jnp.float32) * s2, 'bk': jax.random.normal(ks[5], (E,), jnp.float32) * 0.01, 'Wv': jax.random.normal(ks[6], (D2, E), jnp.float32) * s2, 'bv': jax.random.normal(ks[7], (E,), jnp.float32) * 0.01, 'Wo': jax.random.normal(ks[8], (E, D1), jnp.float32) * se, 'bo': jax.random.normal(ks[9], (D1,), jnp.float32) * 0.01}
    _L0_xattn_all = _L0_xattn_setup()
    _L0_xattn_in = {k: v for k, v in _L0_xattn_all.items() if k in ('ln1_g', 'ln1_b', 'ln2_g', 'ln2_b', 'Wq', 'bq', 'Wk', 'bk', 'Wv', 'bv', 'Wo', 'bo')}
    del _L0_xattn_all

    def _L0_ffn_setup():
        import jax, jax.numpy as jnp
        import numpy as np
        TOP_K = 2
        key = jax.random.key(seed)
        k1, k2, k3, k4 = jax.random.split(key, 4)
        B, T, C = (4, 256, 128)
        E, D_FF = (8, 128)
        x = jax.random.normal(k1, (B, T, C), dtype=jnp.float32)
        router_w = jax.random.normal(k2, (E, C), dtype=jnp.float32) * 0.02
        w1 = jax.random.normal(k3, (E, C, D_FF), dtype=jnp.float32) * 0.02
        w2 = jax.random.normal(k4, (E, D_FF, C), dtype=jnp.float32) * 0.02
        return {'x': x, 'router_w': router_w, 'w1': w1, 'w2': w2}
    _L0_ffn_all = _L0_ffn_setup()
    _L0_ffn_in = {k: v for k, v in _L0_ffn_all.items() if k in ('router_w', 'w1', 'w2')}
    del _L0_ffn_all

    def _L1_xattn_setup():
        import jax, jax.numpy as jnp
        import numpy as np
        HEADS = 8
        DIM_HEAD = 64
        SCALE = DIM_HEAD ** (-0.5)
        key = jax.random.key(seed)
        ks = jax.random.split(key, 7)
        B, Nq, Nc = (4, 256, 256)
        Dq, Dc = (128, 96)
        inner = HEADS * DIM_HEAD
        x = jax.random.normal(ks[0], (B, Nq, Dq), dtype=jnp.float32)
        context = jax.random.normal(ks[1], (B, Nc, Dc), dtype=jnp.float32)
        Wq = jax.random.normal(ks[2], (Dq, inner), dtype=jnp.float32) * Dq ** (-0.5)
        Wk = jax.random.normal(ks[3], (Dc, inner), dtype=jnp.float32) * Dc ** (-0.5)
        Wv = jax.random.normal(ks[4], (Dc, inner), dtype=jnp.float32) * Dc ** (-0.5)
        Wo = jax.random.normal(ks[5], (inner, Dq), dtype=jnp.float32) * inner ** (-0.5)
        bo = jax.random.normal(ks[6], (Dq,), dtype=jnp.float32) * 0.01
        return {'x': x, 'context': context, 'Wq': Wq, 'Wk': Wk, 'Wv': Wv, 'Wo': Wo, 'bo': bo}
    _L1_xattn_all = _L1_xattn_setup()
    _L1_xattn_in = {k: v for k, v in _L1_xattn_all.items() if k in ('Wq', 'Wk', 'Wv', 'Wo', 'bo')}
    del _L1_xattn_all

    def _L1_ffn_setup():
        import jax, jax.numpy as jnp
        import numpy as np
        D_MODEL = 128
        MLP_DIM = 512
        N_EXPERTS = 8
        B, T = (4, 128)
        key = jax.random.key(seed)
        ks = jax.random.split(key, 7)
        scale_in = (1.0 / D_MODEL) ** 0.5
        scale_out = (1.0 / MLP_DIM) ** 0.5
        bound_g = (1.0 / D_MODEL) ** 0.5
        w_gate = jax.random.uniform(ks[0], (D_MODEL, N_EXPERTS), minval=-bound_g, maxval=bound_g, dtype=jnp.float32)
        b_gate = jax.random.uniform(ks[1], (N_EXPERTS,), minval=-bound_g, maxval=bound_g, dtype=jnp.float32)
        W1 = jax.random.uniform(ks[2], (N_EXPERTS, D_MODEL, MLP_DIM), minval=-scale_in, maxval=scale_in, dtype=jnp.float32)
        b1 = jnp.zeros((N_EXPERTS, MLP_DIM), dtype=jnp.float32)
        W2 = jax.random.uniform(ks[3], (N_EXPERTS, MLP_DIM, D_MODEL), minval=-scale_out, maxval=scale_out, dtype=jnp.float32)
        b2 = jnp.zeros((N_EXPERTS, D_MODEL), dtype=jnp.float32)
        x = jax.random.normal(ks[4], (B, T, D_MODEL), dtype=jnp.float32)
        return {'x': x, 'w_gate': w_gate, 'b_gate': b_gate, 'W1': W1, 'b1': b1, 'W2': W2, 'b2': b2}
    _L1_ffn_all = _L1_ffn_setup()
    _L1_ffn_in = {k: v for k, v in _L1_ffn_all.items() if k in ('w_gate', 'b_gate', 'W1', 'b1', 'W2', 'b2')}
    del _L1_ffn_all
    return {'x': x, 'ctx_768': ctx_768, 'g_xattn': g_xattn, 'g_ffn': g_ffn, 'L0_xattn_ln1_g': _L0_xattn_in['ln1_g'], 'L0_xattn_ln1_b': _L0_xattn_in['ln1_b'], 'L0_xattn_ln2_g': _L0_xattn_in['ln2_g'], 'L0_xattn_ln2_b': _L0_xattn_in['ln2_b'], 'L0_xattn_Wq': _L0_xattn_in['Wq'], 'L0_xattn_bq': _L0_xattn_in['bq'], 'L0_xattn_Wk': _L0_xattn_in['Wk'], 'L0_xattn_bk': _L0_xattn_in['bk'], 'L0_xattn_Wv': _L0_xattn_in['Wv'], 'L0_xattn_bv': _L0_xattn_in['bv'], 'L0_xattn_Wo': _L0_xattn_in['Wo'], 'L0_xattn_bo': _L0_xattn_in['bo'], 'L0_ffn_router_w': _L0_ffn_in['router_w'], 'L0_ffn_w1': _L0_ffn_in['w1'], 'L0_ffn_w2': _L0_ffn_in['w2'], 'L1_xattn_Wq': _L1_xattn_in['Wq'], 'L1_xattn_Wk': _L1_xattn_in['Wk'], 'L1_xattn_Wv': _L1_xattn_in['Wv'], 'L1_xattn_Wo': _L1_xattn_in['Wo'], 'L1_xattn_bo': _L1_xattn_in['bo'], 'L1_ffn_w_gate': _L1_ffn_in['w_gate'], 'L1_ffn_b_gate': _L1_ffn_in['b_gate'], 'L1_ffn_W1': _L1_ffn_in['W1'], 'L1_ffn_b1': _L1_ffn_in['b1'], 'L1_ffn_W2': _L1_ffn_in['W2'], 'L1_ffn_b2': _L1_ffn_in['b2']}

def reference(x, ctx_768, g_xattn, g_ffn, L0_xattn_ln1_g, L0_xattn_ln1_b, L0_xattn_ln2_g, L0_xattn_ln2_b, L0_xattn_Wq, L0_xattn_bq, L0_xattn_Wk, L0_xattn_bk, L0_xattn_Wv, L0_xattn_bv, L0_xattn_Wo, L0_xattn_bo, L0_ffn_router_w, L0_ffn_w1, L0_ffn_w2, L1_xattn_Wq, L1_xattn_Wk, L1_xattn_Wv, L1_xattn_Wo, L1_xattn_bo, L1_ffn_w_gate, L1_ffn_b_gate, L1_ffn_W1, L1_ffn_b1, L1_ffn_W2, L1_ffn_b2):
    import jax
    import jax.numpy as jnp

    def _L0_xattn_ref(modality1, modality2, ln1_g, ln1_b, ln2_g, ln2_b, Wq, bq, Wk, bk, Wv, bv, Wo, bo):
        import jax, jax.numpy as jnp
        import numpy as np
        EPS = 1e-05

        def layernorm(x, g, b):
            mu = jnp.mean(x, axis=-1, keepdims=True)
            var = jnp.mean(jnp.square(x - mu), axis=-1, keepdims=True)
            return (x - mu) * jax.lax.rsqrt(var + EPS) * g + b
        E = Wq.shape[1]
        scaling = E ** (-0.5)
        x1 = layernorm(modality1, ln1_g, ln1_b)
        x2 = layernorm(modality2, ln2_g, ln2_b)
        q = x1 @ Wq + bq
        k = x2 @ Wk + bk
        v = x2 @ Wv + bv
        scores = jnp.einsum('bqe,bke->bqk', q, k) * scaling
        attn = jax.nn.softmax(scores, axis=-1)
        ctx = jnp.einsum('bqk,bke->bqe', attn, v)
        return ctx @ Wo + bo

    def _L0_ffn_ref(x, router_w, w1, w2):
        import jax, jax.numpy as jnp
        import numpy as np
        TOP_K = 2
        B, T, C = x.shape
        x_flat = x.reshape(-1, C)
        logits = x_flat @ router_w.T
        probs = jax.nn.softmax(logits, axis=-1)
        weights, indices = jax.lax.top_k(probs, TOP_K)
        hidden = jax.nn.relu(jnp.einsum('nc,ecf->nef', x_flat, w1))
        out_all = jnp.einsum('nef,efc->nec', hidden, w2)
        sel = jnp.take_along_axis(out_all, indices[:, :, None], axis=1)
        out = jnp.sum(sel * weights[:, :, None], axis=1)
        return out.reshape(B, T, C)

    def _L1_xattn_ref(x, context, Wq, Wk, Wv, Wo, bo):
        import jax, jax.numpy as jnp
        import numpy as np
        HEADS = 8
        DIM_HEAD = 64
        SCALE = DIM_HEAD ** (-0.5)
        B, Nq, _ = x.shape
        q = (x @ Wq).reshape(B, Nq, HEADS, DIM_HEAD)
        k = (context @ Wk).reshape(B, context.shape[1], HEADS, DIM_HEAD)
        v = (context @ Wv).reshape(B, context.shape[1], HEADS, DIM_HEAD)
        sim = jnp.einsum('bihd,bjhd->bhij', q, k) * SCALE
        attn = jax.nn.softmax(sim, axis=-1)
        out = jnp.einsum('bhij,bjhd->bihd', attn, v)
        out = out.reshape(B, Nq, HEADS * DIM_HEAD)
        return out @ Wo + bo

    def _L1_ffn_ref(x, w_gate, b_gate, W1, b1, W2, b2):
        import jax, jax.numpy as jnp
        import numpy as np
        D_MODEL = 128
        MLP_DIM = 512
        N_EXPERTS = 8
        B, T = (4, 128)
        b, t, d = x.shape
        x_flat = x.reshape(b * t, d)
        logits = x_flat @ w_gate + b_gate
        probs = jax.nn.softmax(logits, axis=-1)
        route_p = jnp.max(probs, axis=-1)
        route_idx = jnp.argmax(probs, axis=-1)
        h = jnp.einsum('nd,edm->enm', x_flat, W1) + b1[:, None, :]
        h = jax.nn.relu(h)
        y = jnp.einsum('enm,emd->end', h, W2) + b2[:, None, :]
        n = b * t
        out = y[route_idx, jnp.arange(n)] * route_p[:, None]
        return out.reshape(b, t, d)
    x = x + jnp.tanh(g_xattn[0]) * _L0_xattn_ref(_layernorm(x, axis=-1), ctx_768, L0_xattn_ln1_g, L0_xattn_ln1_b, L0_xattn_ln2_g, L0_xattn_ln2_b, L0_xattn_Wq, L0_xattn_bq, L0_xattn_Wk, L0_xattn_bk, L0_xattn_Wv, L0_xattn_bv, L0_xattn_Wo, L0_xattn_bo)
    x = x + jnp.tanh(g_ffn[0]) * _L0_ffn_ref(_layernorm(x, axis=-1), L0_ffn_router_w, L0_ffn_w1, L0_ffn_w2)
    x = x + jnp.tanh(g_xattn[1]) * _L1_xattn_ref(_layernorm(x, axis=-1), ctx_768, L1_xattn_Wq, L1_xattn_Wk, L1_xattn_Wv, L1_xattn_Wo, L1_xattn_bo)
    x = x + jnp.tanh(g_ffn[1]) * _L1_ffn_ref(_layernorm(x, axis=-1), L1_ffn_w_gate, L1_ffn_b_gate, L1_ffn_W1, L1_ffn_b1, L1_ffn_W2, L1_ffn_b2)
    return x

_drawn_inputs = setup_inputs


def setup_inputs(seed=0):
    import zlib

    import numpy as np

    out = dict(_drawn_inputs(seed))
    spreads = {'g_ffn': (-1.0, 0.6),
     'L0_xattn_ln1_g': (1.0, 0.539),
     'L0_xattn_ln1_b': (0.0, 0.638),
     'L0_xattn_ln2_g': (1.0, 0.2),
     'L0_xattn_ln2_b': (0.0, 0.1),
     'L1_ffn_b1': (0.0, 0.8),
     'L1_ffn_b2': (0.0, 0.461)}
    factors = {'L0_xattn_bq': 8.0,
     'L0_xattn_bk': 8.0,
     'L0_xattn_bv': 8.0,
     'L0_xattn_bo': 6.984,
     'L0_ffn_router_w': 8.0,
     'L0_ffn_w1': 8.0,
     'L0_ffn_w2': 8.0,
     'L1_xattn_bo': 6.808,
     'L1_ffn_b_gate': 5.142}
    for name, (base, spread) in spreads.items():
        noise = np.random.default_rng([zlib.crc32(name.encode()), seed]).standard_normal(out[name].shape)
        drawn = base * np.exp(spread * noise) if base else spread * noise
        out[name] = jnp.asarray(drawn.astype(out[name].dtype))
    for name, factor in factors.items():
        out[name] = (out[name] * factor).astype(out[name].dtype)
    return out
```

```python
import concourse.bass as bass
from concourse import mybir
from contextlib import ExitStack

P = 128
EPS = 1e-05
BIG = 1e30

ALU = mybir.AluOpType
ACT = mybir.ActivationFunctionType
AX = mybir.AxisListType
F32 = mybir.dt.float32


def gated_blocks_kernel(nc, A, out):
    B, N, D = A["x"].shape
    NC, DC = A["ctx_768"].shape[1:]
    K = N // P
    T = B * K
    J = B * NC
    X = A["L0_ffn_w1"].shape[0]
    H1, HD = 8, 64
    C1 = H1 * HD // P
    F0, F1 = A["L0_ffn_w1"].shape[2], A["L1_ffn_W1"].shape[2]
    M1 = F1 // P
    SC0, SC1 = float(D) ** -0.5, float(HD) ** -0.5
    assert F0 == P and D == P and NC * K == P and J == 64

    with ExitStack() as ctx:
        def sb(name, shape, dt=F32):
            return ctx.enter_context(nc.sbuf_tensor(name, shape, dt))

        def sem(name):
            return ctx.enter_context(nc.semaphore(name))

        bank = [ctx.enter_context(nc.psum_tensor(f"bank{i}", [P, 512], F32)) for i in range(8)]

        x = sb("x_res", [P, T, D])
        xb = sb("x_plus_bias", [P, T, D])
        z = sb("z", [P, T, D])
        zT = sb("zT", [P, B, N])
        st = sb("stats", [P, T, 6])
        mv = sb("mean_var", [P, T, 2])
        va = sb("var_eps", [P, T])
        rs = sb("rstd", [P, T])
        nhalf = sb("minus_half", [P, T])
        ident = sb("ident", [P, P])
        iota8 = sb("iota8", [P, X])
        mask4 = sb("mask4", [P, 4])
        mask4g = sb("mask4g", [P, 4])
        mask2 = sb("mask2", [P, 2])
        ones = sb("ones", [1, P])
        gates = sb("gates", [P, 4])
        tg = sb("tanh_gates", [P, 4])
        NR = 32 + 5 + X
        rows = sb("param_rows", [NR, P])
        cols = sb("param_cols", [P, NR])
        ln2r = sb("ln2_rows", [2, DC])
        ln2c = sb("ln2_cols", [DC, 2])
        bo0 = sb("bo0", [P, D])
        bo1 = sb("bo1", [P, D])
        cx = sb("ctx", [J, DC])
        cz = sb("ctx_norm", [J, DC])
        cst = sb("ctx_stats", [J, 6])
        cmv = sb("ctx_mean_var", [J, 2])
        cva = sb("ctx_var_eps", [J, 1])
        crs = sb("ctx_rstd", [J, 1])
        cT = sb("ctxT", [DC, J])
        c2T = sb("ctx_normT", [DC, J])
        wq0 = sb("wq0", [D, P])
        wk0 = sb("wk0", [DC, P])
        wv0 = sb("wv0", [DC, P])
        wo0 = sb("wo0", [P, D])
        wq0T = sb("wq0T", [P, D])
        kT0 = sb("kT0", [P, J])
        vT0 = sb("vT0", [P, B, 4, NC])
        kq0 = sb("kq0", [D, J])
        kq0g = sb("kq0g", [D, J])
        c0 = sb("score_bias", [1, B, 4, NC])
        vo0 = sb("vo0", [P, B, 4, D])
        wq1 = sb("wq1", [D, C1, P])
        wk1 = sb("wk1", [DC, C1, P])
        wv1 = sb("wv1", [DC, C1, P])
        wo1 = sb("wo1", [P, C1, D])
        wq1T = sb("wq1T", [P, C1, D])
        kb1 = sb("k_blocks", [P, C1, 2, J])
        vb1 = sb("v_blocks", [P, C1, B, 2, NC])
        kq1 = sb("kq1", [D, B, H1, NC])
        vo1 = sb("vo1", [P, B, 2, D])
        sd = sb("scores_shifted", [P, 2, 512])
        pr = sb("probs", [P, 2, 512])
        pT = sb("probsT", [P, 2, 512])
        mx = sb("row_max", [P, 2, 16])
        sm = sb("row_sum", [P, 2, 16])
        ri = sb("row_inv", [P, 2, 16])
        w01 = sb("w01", [D, X, F0])
        w02 = sb("w02", [F0, X, D])
        w11 = sb("w11", [D, X, F1])
        w12 = sb("w12", [P, X, M1, D])
        wg1 = sb("w_gate", [D, X])
        bg1 = sb("b_gate", [P, X])
        b21 = sb("b2", [X, D])
        h = sb("hidden", [P, 4, N])
        lg = sb("logits", [P, T, X])
        l2 = sb("logits2", [P, T, X])
        ta = sb("cand", [P, T, X])
        oh = sb("onehot", [P, T, X])
        oh2 = sb("onehot2", [P, T, X])
        ex = sb("expl", [P, T, X])
        gt = sb("expert_gate", [P, T, X])
        gT = sb("expert_gateT", [X, T, P])
        m1 = sb("top1", [P, T])
        ix = sb("top_idx", [P, T])
        zs = sb("denom", [P, T])

        made = {}

        def s(name):
            if name not in made:
                made[name] = ctx.enter_context(nc.semaphore(name))
            return made[name]

        block = ctx.enter_context(nc.Block())

        def tok(a, b):
            return a[b].rearrange("(p k) d -> p k d", k=K)

        def half(t, b):
            return t[:, b * K:(b + 1) * K]

        RB, RL, RR = 0, 32, 37

        @block.sync
        def _(sp):
            for b in range(B):
                sp.dma_start(half(x, b), tok(A["x"], b)).then_inc(s(f"x_in{b}"), 16)
            for i, name in enumerate(("ln1_g", "ln1_b", "bq", "bk", "bv")):
                sp.dma_start(rows[RL + i:RL + i + 1, :], A["L0_xattn_" + name].rearrange("(a d) -> a d", a=1)).then_inc(s("rows_in"), 16)
            sp.dma_start(rows[RR:RR + X, :], A["L0_ffn_router_w"]).then_inc(s("rows_in"), 16)
            sp.dma_start(rows[0:32, :], A["L1_ffn_b1"].rearrange("e (c p) -> (e c) p", p=P)).then_inc(s("rows_in"), 16)
            for t, name in ((wq0, "Wq"), (wk0, "Wk"), (wv0, "Wv"), (wo0, "Wo")):
                sp.dma_start(t[:, :], A["L0_xattn_" + name]).then_inc(s("w0_in"), 16)
            sp.dma_start(w01[:, :, :], A["L0_ffn_w1"].rearrange("e c f -> c e f")).then_inc(s("f0_in"), 16)
            sp.dma_start(w02[:, :, :], A["L0_ffn_w2"].rearrange("e f c -> f e c")).then_inc(s("f0_in"), 16)
            for t, name in ((wq1, "Wq"), (wk1, "Wk"), (wv1, "Wv")):
                sp.dma_start(t[:, :, :], A["L1_xattn_" + name].rearrange("d (c n) -> d c n", c=C1)).then_inc(s("w1_in"), 16)
            sp.dma_start(wo1[:, :, :], A["L1_xattn_Wo"].rearrange("(c p) d -> p c d", p=P)).then_inc(s("w1_in"), 16)
            sp.dma_start(w11[:, :, :], A["L1_ffn_W1"].rearrange("e d m -> d e m")).then_inc(s("f1_in"), 16)
            sp.dma_start(w12[:, :, :, :], A["L1_ffn_W2"].rearrange("e (c p) d -> p e c d", p=P)).then_inc(s("f1_in"), 16)
            for b in range(B):
                sp.wait_ge(s("x4"), b + 1)
                sp.dma_start(tok(out, b), half(x, b)).then_inc(s("stored"), 16)
            sp.wait_ge(s("stored"), 16 * B)

        @block.gpsimd
        def _(pool):
            row = lambda a: a.rearrange("(a d) -> a d", a=1)
            pool.dma_start(gates[:, 0:2], row(A["g_xattn"]).to_broadcast([P, 2])).then_inc(s("gates_in"), 16)
            pool.dma_start(gates[:, 2:4], row(A["g_ffn"]).to_broadcast([P, 2])).then_inc(s("gates_in"), 16)
            pool.dma_start(cx[:, :], A["ctx_768"].rearrange("b n d -> (b n) d")).then_inc(s("ctx_in"), 16)
            pool.dma_start(ln2r[0:1, :], row(A["L0_xattn_ln2_g"])).then_inc(s("ln2_in"), 16)
            pool.dma_start(ln2r[1:2, :], row(A["L0_xattn_ln2_b"])).then_inc(s("ln2_in"), 16)
            pool.dma_start(bo0[:, :], row(A["L0_xattn_bo"]).to_broadcast([P, D])).then_inc(s("bo_in"), 16)
            pool.dma_start(bo1[:, :], row(A["L1_xattn_bo"]).to_broadcast([P, D])).then_inc(s("bo_in"), 16)
            pool.dma_start(wg1[:, :], A["L1_ffn_w_gate"]).then_inc(s("gate_w_in"), 16)
            pool.dma_start(bg1[:, :], row(A["L1_ffn_b_gate"]).to_broadcast([P, X])).then_inc(s("gate_w_in"), 16)
            pool.dma_start(b21[:, :], A["L1_ffn_b2"]).then_inc(s("gate_w_in"), 16)
            pool.memset(nhalf[:, :], -0.5)
            pool.memset(ones[:, :], 1.0)
            pool.memset(mask4[:, :], 1.0)
            pool.memset(mask2[:, :], 1.0)
            pool.iota(iota8[:, :], [[1, X]], base=0, channel_multiplier=0, allow_small_or_imprecise_dtypes=True)
            pool.memset(ident[:, :], 0.0).then_inc(s("const_set"), 1)
            pool.wait_ge(s("const_set"), 1)
            pool.affine_select(out=ident[:, :], in_=ident[:, :], compare_op=ALU.not_equal, fill=1.0, base=0,
                               pattern=[[-1, P]], channel_multiplier=1)
            pool.affine_select(out=mask4[:, :], in_=mask4[:, :], compare_op=ALU.is_ge, fill=0.0, base=0,
                               pattern=[[-NC, 4]], channel_multiplier=1)
            pool.affine_select(out=mask2[:, :], in_=mask2[:, :], compare_op=ALU.is_ge, fill=0.0, base=0,
                               pattern=[[-HD, 2]], channel_multiplier=1).then_inc(s("const_set"), 1)
            pool.wait_ge(s("const_set"), 2)
            pool.affine_select(out=mask4[:, :], in_=mask4[:, :], compare_op=ALU.is_ge, fill=0.0, base=NC - 1,
                               pattern=[[NC, 4]], channel_multiplier=-1)
            pool.affine_select(out=mask2[:, :], in_=mask2[:, :], compare_op=ALU.is_ge, fill=0.0, base=HD - 1,
                               pattern=[[HD, 2]], channel_multiplier=-1).then_inc(s("consts"), 1)
            pool.wait_ge(s("consts"), 1)
            pool.wait_ge(s("cvar"), 1)
            pool.tensor_tensor(crs[:, :], cva[:, :], nhalf[0:J, 0:1], ALU.pow).then_inc(s("crstd"), 1)
            for i in range(4):
                for b in range(B):
                    pool.wait_ge(s("var"), i * B + b + 1)
                    pool.tensor_tensor(half(rs, b), half(va, b), half(nhalf, b), ALU.pow).then_inc(s("rstd"), 1)
                if i in (0, 2):
                    if i == 0:
                        pool.wait_ge(s("bo_tanh"), 1)
                    bo = bo0 if i == 0 else bo1
                    for b in range(B):
                        pool.tensor_tensor(half(xb, b), half(x, b), bo[:, :].unsqueeze(1).to_broadcast([P, K, D]), ALU.add).then_inc(s("xb"), 1)

        @block.scalar
        def _(act):
            act.wait_ge(s("gates_in"), 32)
            nc.scalar.activation(tg[:, :], gates[:, :], ACT.Tanh).then_inc(s("tanh"), 1)
            for b in range(B):
                act.wait_ge(s("shift0"), b + 1)
                nc.scalar.activation(pr[:, b, 0:P], sd[:, b, 0:P], ACT.Exp, scale=SC0).then_inc(s("exp0"), 1)
            for b in range(B):
                act.wait_ge(s("zT_ps"), 1 * B + b + 1)
                nc.scalar.copy(zT[:, b, :], bank[b][:, :]).then_inc(s("zT"), 1)
            act.wait_ge(s("lshift"), 1)
            nc.scalar.activation(ex[:, :, :], ta[:, :, :], ACT.Exp).then_inc(s("lexp"), 1)
            for i in range(X * B):
                act.wait_ge(s("h_ps"), i + 1)
                if i >= 2:
                    act.wait_ge(s("y_ps"), i - 1)
                nc.scalar.activation(h[:, i % 2, 0:512], bank[2 + i % 2][:, :], ACT.Relu).then_inc(s("h"), 1)
            for b in range(B):
                act.wait_ge(s("zT_ps"), 2 * B + b + 1)
                nc.scalar.copy(zT[:, b, :], bank[b][:, :]).then_inc(s("zT"), 1)
            for q in range(T // 2):
                act.wait_ge(s("shift1"), q + 1)
                nc.scalar.activation(pr[:, q % 2, :], sd[:, q % 2, :], ACT.Exp, scale=SC1).then_inc(s("exp1"), 1)
            for b in range(B):
                act.wait_ge(s("zT_ps"), 3 * B + b + 1)
                nc.scalar.copy(zT[:, b, :], bank[b][:, :]).then_inc(s("zT"), 1)
            act.wait_ge(s("lshift"), 2)
            nc.scalar.activation(ex[:, :, :], ta[:, :, :], ACT.Exp).then_inc(s("lexp"), 1)
            for i in range(X * B):
                for c in range(M1):
                    j = i * M1 + c
                    act.wait_ge(s("h1_ps"), j + 1)
                    if j >= 4:
                        act.wait_ge(s("h1_used"), j - 3)
                    nc.scalar.activation(h[:, j % 4, 0:512], bank[2 + j % 2][:, :], ACT.Relu,
                                         bias=cols[:, (i // B) * M1 + c:(i // B) * M1 + c + 1]).then_inc(s("h1"), 1)

        @block.tensor
        def _(pe):
            mm, tr = nc.tensor.matmul, nc.tensor.transpose
            pe.wait_ge(s("consts"), 1)
            pe.wait_ge(s("rows_in"), 16 * 7)
            tr(bank[6][:, 0:NR], rows[:, :], ident[0:NR, 0:NR])
            pe.wait_ge(s("ln2_in"), 32)
            tr(bank[6][0:DC, 192:194], ln2r[:, :], ident[0:2, 0:2])
            pe.wait_ge(s("w0_in"), 64)
            tr(bank[6][:, 64:192], wq0[:, :], ident[:, :])
            pe.wait_ge(s("ctx_in"), 16)
            tr(bank[6][0:DC, 256:320], cx[:, :], ident[0:J, 0:J])
            pe.wait_ge(s("cz"), 1)
            tr(bank[6][0:DC, 320:384], cz[:, :], ident[0:J, 0:J]).then_inc(s("ctx_tr"), 1)
            pe.wait_ge(s("ctx_T"), 1)
            mm(bank[7][:, 0:J], wk0[:, :], c2T[:, :], start=True, stop=True)
            mm(bank[7][:, J:2 * J], wv0[:, :], c2T[:, :], start=True, stop=True).then_inc(s("kv0_ps"), 1)
            pe.wait_ge(s("kv0"), 1)
            mm(bank[5][:, 0:J], wq0T[:, :], kT0[:, :], start=True, stop=True).then_inc(s("kq0_ps"), 1)
            for b in range(B):
                last = mm(bank[6][:, b * D:(b + 1) * D], vT0[:, b], wo0[:, :], start=True, stop=True)
            last.then_inc(s("vo0_ps"), 1)
            pe.wait_ge(s("kq0"), 1)
            mm(bank[7][0:1, 192:192 + J], cols[:, RL + 1:RL + 2], kq0[:, :], start=True, stop=False)
            mm(bank[7][0:1, 192:192 + J], cols[:, RL + 2:RL + 3], kT0[:, :], start=False, stop=True).then_inc(s("c0_ps"), 1)

            def transpose_z(i, b):
                pe.wait_ge(s("z"), i * B + b + 1)
                for k in range(K):
                    last = tr(bank[b][:, k * P:(k + 1) * P], z[:, b * K + k, :], ident[:, :])
                last.then_inc(s("zT_ps"), 1)

            for b in range(B):
                transpose_z(0, b)
            for b in range(B):
                pe.wait_ge(s("c0"), 1)
                pe.wait_ge(s("zT"), b + 1)
                mm(bank[2 + b][:, 0:P], ones[:, :], c0[0:1, b], start=True, stop=True)
                for k in range(K):
                    last = mm(bank[2 + b][:, k * NC:(k + 1) * NC], zT[:, b, k * P:(k + 1) * P],
                              kq0g[:, b * NC:(b + 1) * NC], start=False, stop=True, skip_group_check=True)
                last.then_inc(s("s0_ps"), 1)
            for b in range(B):
                pe.wait_ge(s("p0"), b + 1)
                tr(bank[2 + b][:, P:2 * P], pr[:, b, 0:P], ident[:, :]).then_inc(s("pT0_ps"), 1)
            for b in range(B):
                pe.wait_ge(s("pT0"), b + 1)
                mm(bank[b][:, :], pT[:, b, 0:P], vo0[:, b], start=True, stop=True).then_inc(s("o0_ps"), 1)
            for b in range(B):
                transpose_z(1, b)
            for b in range(B):
                pe.wait_ge(s("zT"), 1 * B + b + 1)
                for k in range(K):
                    last = mm(bank[7][:, (b * K + k) * X:(b * K + k + 1) * X], zT[:, b, k * P:(k + 1) * P], cols[:, RR:RR + X], start=True, stop=True)
            last.then_inc(s("lg_ps"), 1)
            pe.wait_ge(s("f0_in"), 32)

            def up0(i):
                e, b = i // B, i % B
                if i >= 2:
                    pe.wait_ge(s("h"), i - 1)
                mm(bank[2 + i % 2][:, :], w01[:, e, :], zT[:, b, :], start=True, stop=True).then_inc(s("h_ps"), 1)

            def down0(i):
                e, b = i // B, i % B
                pe.wait_ge(s("h"), i + 1)
                if i >= 2:
                    pe.wait_ge(s("y_used"), i - 1)
                for k in range(K):
                    last = mm(bank[4 + i % 2][:, k * D:(k + 1) * D], h[:, i % 2, k * P:(k + 1) * P], w02[:, e, :], start=True, stop=True)
                last.then_inc(s("y_ps"), 1)

            up0(0)
            for i in range(X * B):
                if i + 1 < X * B:
                    up0(i + 1)
                down0(i)

            pe.wait_ge(s("w1_in"), 64)
            pe.wait_ge(s("y_used"), X * B)
            for c in range(C1):
                last = tr(bank[5][:, c * P:(c + 1) * P], wq1[:, c, :], ident[:, :])
            last.then_inc(s("wq1T_ps"), 1)
            for c in range(C1):
                mm(bank[4][:, c * J:(c + 1) * J], wk1[:, c, :], cT[:, :], start=True, stop=True)
            for c in range(C1):
                last = mm(bank[4][:, 256 + c * J:256 + (c + 1) * J], wv1[:, c, :], cT[:, :], start=True, stop=True)
            last.then_inc(s("kv1_ps"), 1)
            pe.wait_ge(s("kv1"), 1)
            for c in range(C1):
                last = mm(bank[5][:, c * P:(c + 1) * P], wq1T[:, c, :], kb1[:, c], start=True, stop=True)
            last.then_inc(s("kq1_ps"), 1)
            for b in range(B):
                for c in range(C1):
                    r = 64 * (c % 2)
                    at = (b * 2 + c // 2) * D
                    last = mm(bank[4][r:r + 64, at:at + D], vb1[:, c, b], wo1[:, c, :], start=True, stop=True)
            last.then_inc(s("vo1_ps"), 1)

            for b in range(B):
                transpose_z(2, b)
            pe.wait_ge(s("vo1"), 1)

            def scores1(q):
                b = q // 2
                if q >= 2:
                    pe.wait_ge(s("shift1"), q - 1)
                pe.wait_ge(s("zT"), 2 * B + b + 1)
                for u in range(2):
                    k = (q % 2) * 2 + u
                    last = mm(bank[2 + q % 2][:, u * 256:(u + 1) * 256], zT[:, b, k * P:(k + 1) * P], kq1[:, b], start=True, stop=True)
                last.then_inc(s("s1_ps"), 1)

            def mix1(q):
                b = q // 2
                pe.wait_ge(s("p1"), q + 1)
                for u in range(4):
                    last = tr(bank[4 + q % 2][:, u * P:(u + 1) * P], pr[:, q % 2, u * P:(u + 1) * P], ident[:, :])
                last.then_inc(s("pT1_ps"), 1)
                pe.wait_ge(s("pT1"), q + 1)
                if q >= 2:
                    pe.wait_ge(s("x3"), q - 1)
                for u in range(2):
                    for g in range(2):
                        last = mm(bank[6 + q % 2][:, u * D:(u + 1) * D], pT[:, q % 2, (u * 2 + g) * P:(u * 2 + g + 1) * P],
                                  vo1[:, b, g, :], start=g == 0, stop=g == 1)
                last.then_inc(s("o1_ps"), 1)

            scores1(0)
            for q in range(T // 2):
                if q + 1 < T // 2:
                    scores1(q + 1)
                mix1(q)
            for b in range(B):
                transpose_z(3, b)
            for b in range(B):
                pe.wait_ge(s("zT"), 3 * B + b + 1)
                pe.wait_ge(s("gate_w_in"), 48)
                for k in range(K):
                    last = mm(bank[7][:, (b * K + k) * X:(b * K + k + 1) * X], zT[:, b, k * P:(k + 1) * P], wg1[:, :], start=True, stop=True)
            last.then_inc(s("lg_ps"), 1)
            pe.wait_ge(s("gate1"), 1)
            for b in range(B):
                for k in range(K):
                    last = tr(bank[6 + b][0:X, k * P:(k + 1) * P], gt[:, b * K + k, :], ident[:, :])
                last.then_inc(s("gT_ps"), 1)
            for b in range(B):
                pe.wait_ge(s("gT"), b + 1)
                for k in range(K):
                    last = mm(bank[6 + b][:, k * D:(k + 1) * D], gT[:, b * K + k, :], b21[:, :], start=True, stop=True)
                last.then_inc(s("b2_ps"), 1)
            pe.wait_ge(s("f1_in"), 32)

            def up1(j):
                i, c = j // M1, j % M1
                e, b = i // B, i % B
                if j >= 2:
                    pe.wait_ge(s("h1"), j - 1)
                mm(bank[2 + j % 2][:, :], w11[:, e, c * P:(c + 1) * P], zT[:, b, :], start=True, stop=True).then_inc(s("h1_ps"), 1)

            def down1(j):
                i, c = j // M1, j % M1
                e = i // B
                pe.wait_ge(s("h1"), j + 1)
                if c == 0 and i >= 2:
                    pe.wait_ge(s("y1_used"), i - 1)
                for k in range(K):
                    last = mm(bank[4 + i % 2][:, k * D:(k + 1) * D], h[:, j % 4, k * P:(k + 1) * P], w12[:, e, c, :],
                              start=c == 0 and k == 0, stop=c == M1 - 1, skip_group_check=True)
                last.then_inc(s("h1_used"), 1)

            up1(0)
            for j in range(X * B * M1):
                if j + 1 < X * B * M1:
                    up1(j + 1)
                down1(j)

        @block.vector
        def _(dve):
            v = nc.vector
            step = [0]

            def link(ins):
                step[0] += 1
                ins.then_inc(s("dve_step"), 1)
                dve.wait_ge(s("dve_step"), step[0])

            def bc(a, shape):
                return a.unsqueeze(len(a.shape)).to_broadcast(shape)

            def norm(i, b):
                for k in range(K):
                    last = v.bn_stats(st[:, b * K + k, :], x[:, b * K + k, :])
                link(last)
                for k in range(K):
                    last = v.bn_aggr(mv[:, b * K + k, :], st[:, b * K + k, :])
                link(last)
                if i == 0:
                    v.tensor_scalar(half(va, b), mv[:, b * K:(b + 1) * K, 1], 1.0 + EPS, EPS * EPS, ALU.mult, ALU.add).then_inc(s("var"), 1)
                else:
                    v.tensor_scalar(half(va, b), mv[:, b * K:(b + 1) * K, 1], EPS, None, ALU.add).then_inc(s("var"), 1)

            def apply(i, b):
                dve.wait_ge(s("rstd"), i * B + b + 1)
                for k in range(K):
                    t = b * K + k
                    last = v.tensor_scalar(z[:, t, :], x[:, t, :], mv[:, t, 0:1], rs[:, t:t + 1], ALU.subtract, ALU.mult)
                last.then_inc(s("z"), 1)

            dve.wait_ge(s("ctx_in"), 16)
            link(v.bn_stats(cst[:, :], cx[:, :]))
            link(v.bn_aggr(cmv[:, :], cst[:, :]))
            v.tensor_scalar(cva[:, :], cmv[:, 1:2], EPS, None, ALU.add).then_inc(s("cvar"), 1)
            dve.wait_ge(s("crstd"), 1)
            v.tensor_scalar(cz[:, :], cx[:, :], cmv[:, 0:1], crs[:, 0:1], ALU.subtract, ALU.mult).then_inc(s("cz"), 1)
            for b in range(B):
                dve.wait_ge(s(f"x_in{b}"), 16)
                norm(0, b)
            for b in range(B):
                apply(0, b)
            dve.wait_ge(s("ctx_tr"), 1)
            v.tensor_copy(cT[:, :], bank[6][0:DC, 256:320])
            v.tensor_copy(wq0T[:, :], bank[6][:, 64:192])
            v.tensor_copy(cols[:, :], bank[6][:, 0:NR])
            link(v.tensor_copy(ln2c[:, :], bank[6][0:DC, 192:194]))
            v.tensor_scalar(c2T[:, :], bank[6][0:DC, 320:384], ln2c[:, 0:1], ln2c[:, 1:2], ALU.mult, ALU.add).then_inc(s("ctx_T"), 1)
            dve.wait_ge(s("tanh"), 1)
            v.tensor_scalar(mask4g[:, :], mask4[:, :], tg[:, 0:1], None, ALU.mult)
            dve.wait_ge(s("bo_in"), 32)
            v.tensor_scalar(bo0[:, :], bo0[:, :], tg[:, 0:1], None, ALU.mult)
            v.tensor_scalar(bo1[:, :], bo1[:, :], tg[:, 1:2], None, ALU.mult).then_inc(s("bo_tanh"), 1)
            dve.wait_ge(s("kv0_ps"), 1)
            v.tensor_scalar(kT0[:, :], bank[7][:, 0:J], cols[:, RL + 3:RL + 4], None, ALU.add)
            v.tensor_scalar(vT0[:, :, :, :], bank[7][:, J:2 * J].rearrange("p (b j) -> p b j", b=B).unsqueeze(2).to_broadcast([P, B, 4, NC]),
                            cols[:, RL + 4:RL + 5], None, ALU.add).then_inc(s("kv0"), 1)
            dve.wait_ge(s("kq0_ps"), 1)
            v.tensor_copy(kq0[:, :], bank[5][:, 0:J])
            v.tensor_scalar(kq0g[:, :], bank[5][:, 0:J], cols[:, RL:RL + 1], None, ALU.mult).then_inc(s("kq0"), 1)
            dve.wait_ge(s("vo0_ps"), 1)
            for b in range(B):
                v.tensor_tensor(vo0[:, b], bank[6][:, b * D:(b + 1) * D].unsqueeze(1).to_broadcast([P, 4, D]),
                                bc(mask4g[:, :], [P, 4, D]), ALU.mult)
            dve.wait_ge(s("c0_ps"), 1)
            v.tensor_copy(c0[:, :, :, :], bank[7][0:1, 192:192 + J].rearrange("p (b j) -> p b j", b=B).unsqueeze(2).to_broadcast([1, B, 4, NC])).then_inc(s("c0"), 1)
            for b in range(B):
                dve.wait_ge(s("zT_ps"), b + 1)
                v.tensor_copy(zT[:, b, :], bank[b][:, :]).then_inc(s("zT"), 1)

            def softmax(S, q, G, w, shift, expd, done, count):
                sq, pq = (t[:, q, 0:G * w].rearrange("p (g w) -> p g w", g=G) for t in (sd, pr))
                m, u, r = mx[:, q, 0:G], sm[:, q, 0:G], ri[:, q, 0:G]
                link(v.tensor_reduce(m, S, AX.X, ALU.max))
                v.tensor_tensor(sq, S, bc(m, [P, G, w]), ALU.subtract).then_inc(s(shift), 1)
                dve.wait_ge(s(expd), count)
                link(v.tensor_reduce(u, pq, AX.X, ALU.add))
                link(v.reciprocal(r, u))
                v.tensor_tensor(pq, pq, bc(r, [P, G, w]), ALU.mult).then_inc(s(done), 1)

            for b in range(B):
                dve.wait_ge(s("s0_ps"), b + 1)
                softmax(bank[2 + b][:, 0:P].rearrange("p (k j) -> p k j", k=K), b, K, NC, "shift0", "exp0", "p0", b + 1)
            for b in range(B):
                dve.wait_ge(s("pT0_ps"), b + 1)
                v.tensor_copy(pT[:, b, 0:P], bank[2 + b][:, P:2 * P]).then_inc(s("pT0"), 1)
            for b in range(B):
                dve.wait_ge(s("o0_ps"), b + 1)
                dve.wait_ge(s("xb"), b + 1)
                link(v.tensor_tensor(half(x, b), bank[b][:, :].rearrange("p (k d) -> p k d", k=K), half(xb, b), ALU.add))
                norm(1, b)
            for b in range(B):
                apply(1, b)

            def first_max(src):
                full = [P, T, X]
                lowest = iota8[:, :].unsqueeze(1).to_broadcast(full)
                link(v.tensor_reduce(m1[:, :], src[:, :, :], AX.X, ALU.max))
                link(v.tensor_tensor(ta[:, :, :], src[:, :, :], bc(m1[:, :], full), ALU.not_equal))
                link(v.scalar_tensor_tensor(ta[:, :, :], ta[:, :, :], float(X), lowest, ALU.mult, ALU.add))
                link(v.tensor_reduce(ix[:, :], ta[:, :, :], AX.X, ALU.min))
                return lowest, bc(ix[:, :], full)

            def gate(layer):
                full = [P, T, X]
                dve.wait_ge(s("lg_ps"), layer + 1)
                ps = bank[7][:, 0:T * X].rearrange("p (t e) -> p t e", t=T)
                if layer == 0:
                    link(v.tensor_copy(lg[:, :, :], ps))
                else:
                    dve.wait_ge(s("gate_w_in"), 48)
                    link(v.tensor_tensor(lg[:, :, :], ps, bg1[:, :].unsqueeze(1).to_broadcast(full), ALU.add))
                a, c = first_max(lg)
                link(v.tensor_tensor(oh[:, :, :], a, c, ALU.is_equal))
                link(v.tensor_tensor(ta[:, :, :], lg[:, :, :], bc(m1[:, :], full), ALU.subtract))
                v.tensor_copy(ta[:, :, :], ta[:, :, :]).then_inc(s("lshift"), 1)
                dve.wait_ge(s("lexp"), layer + 1)
                if layer == 0:
                    link(v.scalar_tensor_tensor(l2[:, :, :], oh[:, :, :], -BIG, lg[:, :, :], ALU.mult, ALU.add))
                    a, c = first_max(l2)
                    link(v.tensor_tensor(oh2[:, :, :], a, c, ALU.is_equal))
                    link(v.tensor_tensor(oh[:, :, :], oh[:, :, :], oh2[:, :, :], ALU.add))
                link(v.tensor_reduce(zs[:, :], ex[:, :, :], AX.X, ALU.add))
                link(v.reciprocal(zs[:, :], zs[:, :]))
                link(v.tensor_scalar(zs[:, :], zs[:, :], tg[:, 2 + layer:3 + layer], None, ALU.mult))
                link(v.tensor_tensor(gt[:, :, :], ex[:, :, :], oh[:, :, :], ALU.mult))
                v.tensor_tensor(gt[:, :, :], gt[:, :, :], bc(zs[:, :], full), ALU.mult).then_inc(s(f"gate{layer}"), 1)
                dve.wait_ge(s(f"gate{layer}"), 1)

            gate(0)
            for i in range(X * B):
                e, b = i // B, i % B
                dve.wait_ge(s("y_ps"), i + 1)
                if b == 0 and e:
                    dve.wait_ge(s("y_used"), i)
                for k in range(K):
                    t = b * K + k
                    last = v.scalar_tensor_tensor(x[:, t, :], bank[4 + i % 2][:, k * D:(k + 1) * D], gt[:, t, e:e + 1], x[:, t, :], ALU.mult, ALU.add)
                last.then_inc(s("y_used"), 1)
            dve.wait_ge(s("y_used"), X * B)
            for b in range(B):
                norm(2, b)
            for b in range(B):
                apply(2, b)
            dve.wait_ge(s("wq1T_ps"), 1)
            v.tensor_copy(wq1T[:, :, :], bank[5][:, :].rearrange("p (c d) -> p c d", c=C1))
            dve.wait_ge(s("kv1_ps"), 1)
            for hh in range(2):
                v.tensor_scalar(kb1[:, :, hh, :], bank[4][:, 0:256].rearrange("p (c j) -> p c j", c=C1), mask2[:, hh:hh + 1], None, ALU.mult)
            for hh in range(2):
                last = v.tensor_scalar(vb1[:, :, :, hh, :], bank[4][:, 256:512].rearrange("p (c b j) -> p c b j", c=C1, b=B), mask2[:, hh:hh + 1], None, ALU.mult)
            last.then_inc(s("kv1"), 1)
            dve.wait_ge(s("kq1_ps"), 1)
            for b in range(B):
                v.tensor_copy(kq1[:, b], bank[5][:, :].rearrange("p (h b j) -> p h b j", h=H1, b=B)[:, :, b, :])
            dve.wait_ge(s("vo1_ps"), 1)
            v.tensor_scalar(vo1[:, :, :, :].rearrange("p b g d -> p (b g d)"), bank[4][:, :], tg[:, 1:2], None, ALU.mult).then_inc(s("vo1"), 1)

            for q in range(T // 2):
                dve.wait_ge(s("s1_ps"), q + 1)
                if q >= 2:
                    dve.wait_ge(s("pT1_ps"), q - 1)
                softmax(bank[2 + q % 2][:, :].rearrange("p (g j) -> p g j", j=NC), q % 2, 16, NC, "shift1", "exp1", "p1", q + 1)
                dve.wait_ge(s("pT1_ps"), q + 1)
                v.tensor_copy(pT[:, q % 2, :], bank[4 + q % 2][:, :]).then_inc(s("pT1"), 1)
                dve.wait_ge(s("o1_ps"), q + 1)
                dve.wait_ge(s("xb"), B + q // 2 + 1)
                v.tensor_tensor(x[:, 2 * q:2 * q + 2, :], bank[6 + q % 2][:, 0:2 * D].rearrange("p (u d) -> p u d", u=2),
                                xb[:, 2 * q:2 * q + 2, :], ALU.add).then_inc(s("x3"), 1)
            dve.wait_ge(s("x3"), T // 2)
            for b in range(B):
                norm(3, b)
            for b in range(B):
                apply(3, b)
            gate(1)
            for b in range(B):
                dve.wait_ge(s("gT_ps"), b + 1)
                v.tensor_copy(gT[:, b * K:(b + 1) * K, :], bank[6 + b][0:X, :].rearrange("p (k t) -> p k t", k=K)).then_inc(s("gT"), 1)
            for b in range(B):
                dve.wait_ge(s("b2_ps"), b + 1)
                link(v.tensor_tensor(half(x, b), bank[6 + b][:, :].rearrange("p (k d) -> p k d", k=K), half(x, b), ALU.add))
            for i in range(X * B):
                e, b = i // B, i % B
                dve.wait_ge(s("h1_used"), (i + 1) * M1)
                if i:
                    dve.wait_ge(s("y1_used"), min(i, (X - 1) * B))
                for k in range(K):
                    t = b * K + k
                    last = v.scalar_tensor_tensor(x[:, t, :], bank[4 + i % 2][:, k * D:(k + 1) * D], gt[:, t, e:e + 1], x[:, t, :], ALU.mult, ALU.add)
                last.then_inc(s("x4" if e == X - 1 else "y1_used"), 1)


_OUT = ((2, 512, 128), "float32")


def kernel(**inputs):
    import numpy as _np
    import concourse.bacc as _bacc
    from concourse import mybir as _mybir
    from concourse.bass_utils import run_bass_kernel_spmd as _run

    nc = _bacc.Bacc("TRN2", target_bir_lowering=False, num_devices=1)
    arrays, args = {}, {}
    for name, value in inputs.items():
        a = _np.ascontiguousarray(value)
        arrays[f"in_{name}_dram"] = a
        args[name] = nc.dram_tensor(f"in_{name}_dram", a.shape, _mybir.dt.from_np(a.dtype), kind="ExternalInput").ap()
    out = nc.dram_tensor("out_0_dram", _OUT[0], _mybir.dt.from_np(_np.dtype(_OUT[1])), kind="ExternalOutput").ap()
    gated_blocks_kernel(nc, args, out)
    r = _run(nc, [arrays], core_ids=[0])
    return r.results[0]["out_0_dram"]
```

```python
import concourse.bass as bass
from concourse import mybir
from contextlib import ExitStack

P = 128
EPS = 1e-05
HALF_RANGE = 2048

ALU = mybir.AluOpType
ACT = mybir.ActivationFunctionType
AX = mybir.AxisListType
F32 = mybir.dt.float32
F16 = mybir.dt.float16
I32 = mybir.dt.int32
U32 = mybir.dt.uint32

EARLY = (("ident", 128), ("ctx", 96), ("ctxT", 64), ("gates", 4), ("vecs", 7), ("mask4", 4), ("mask2", 2),
         ("wk0", 128), ("wv0", 128), ("wq0T", 128), ("wo0", 128), ("bo0", 128), ("bo1", 128))
LATE = (("routerT", 8), ("w_gate", 8), ("b_gate", 8), ("b1", 32), ("b2", 128), ("before", 128), ("iota8", 8),
        ("before8", 64), ("thresholds", 64), ("tile_starts", 120))


def offsets(table):
    at, out = 0, {}
    for name, width in table:
        out[name] = (at, at + width)
        at += width
    return out, at


def gated_blocks_kernel(nc, A, out):
    B, N, D = A["x"].shape
    NC, DC = 32, 96
    K = N // P
    T = B * K
    J = B * NC
    X = 8
    H1, HD = 8, 64
    C1 = H1 * HD // P
    F1 = 512
    M1 = F1 // P
    TS = T + X - 1
    S = TS * P
    GT = 4
    NG = -(-TS // GT)
    SC0, SC1 = float(D) ** -0.5, float(HD) ** -0.5
    assert S <= HALF_RANGE

    with ExitStack() as ctx:
        def sb(name, shape, dt=F32):
            return ctx.enter_context(nc.sbuf_tensor(name, shape, dt))

        bank = [ctx.enter_context(nc.psum_tensor(f"bank{i}", [P, 512], F32)) for i in range(8)]

        eo, ew = offsets(EARLY)
        lo_, lw = offsets(LATE)
        early = sb("early", [P, ew])
        late = sb("late", [P, lw])

        def E(name, rows=P):
            a, b = eo[name]
            return early[0:rows, a:b]

        def Lt(name, rows=P):
            a, b = lo_[name]
            return late[0:rows, a:b]

        ident = E("ident")
        x = sb("x_res", [P, T, D])
        xb = sb("x_plus_bias", [P, T, D])
        z = sb("z", [P, T, D])
        zTh = sb("zT_hi", [P, B, N], F16)
        zTl = sb("zT_lo", [P, B, N], F16)
        st = sb("stats", [P, T, 6])
        mv = sb("mean_var", [P, T, 2])
        va = sb("var_eps", [P, T])
        rs = sb("rstd", [P, T])
        nhalf = sb("minus_half", [P, T])
        mask4g = sb("mask4g", [P, 4])
        onesf = sb("ones_row", [1, P], F16)
        tg = sb("tanh_gates", [P, 4])
        bog = sb("bias_gated", [P, 2, D])
        cz = sb("ctx_norm", [J, DC])
        cst = sb("ctx_stats", [J, 6])
        cmv = sb("ctx_mean_var", [J, 2])
        cva = sb("ctx_var_eps", [J, 1])
        crs = sb("ctx_rstd", [J, 1])
        c2T = sb("ctx_normT", [DC, J])
        kT0 = sb("kT0", [P, J])
        vT0 = sb("vT0", [P, B, 4, NC])
        kq0 = sb("kq0", [D, J])
        kq0g = sb("kq0g", [D, J])
        kq0h = sb("kq0_hi", [D, J], F16)
        kq0l = sb("kq0_lo", [D, J], F16)
        c0f = sb("score_bias", [1, J])
        c0h = sb("score_bias_hi", [1, B, 4, NC], F16)
        c0l = sb("score_bias_lo", [1, B, 4, NC], F16)
        vo0 = sb("vo0", [P, B, 4, D])
        vo0h = sb("vo0_hi", [P, B, 4, D], F16)
        vo0l = sb("vo0_lo", [P, B, 4, D], F16)
        lay1 = sb("attn1_weights", [P, 4, 512])
        kb1 = sb("k_blocks", [P, C1, 2, J])
        vb1 = sb("v_blocks", [P, C1, B, 2, NC])
        kq1 = sb("kq1", [D, B, H1 * NC])
        kq1h = sb("kq1_hi", [D, B, H1 * NC], F16)
        kq1l = sb("kq1_lo", [D, B, H1 * NC], F16)
        vo1 = sb("vo1", [P, B, 2, D])
        vo1h = sb("vo1_hi", [P, B, 2, D], F16)
        vo1l = sb("vo1_lo", [P, B, 2, D], F16)
        sd = sb("scores_shifted", [P, 2, 512])
        pr = sb("probs", [P, 2, 512])
        pTh = sb("probsT_hi", [P, 2, 512], F16)
        pTl = sb("probsT_lo", [P, 2, 512], F16)
        mx = sb("row_max", [P, 2, 16])
        sm = sb("row_sum", [P, 2, 16])
        ri = sb("row_inv", [P, 2, 16])
        w0 = sb("w0", [P, 2, X * P])
        w0h = sb("w0_hi", [P, 2, X * P], F16)
        w0l = sb("w0_lo", [P, 2, X * P], F16)
        w1 = sb("w1", [P, 2, X * F1])
        w1h = sb("w1_hi", [P, 2, X * F1], F16)
        w1l = sb("w1_lo", [P, 2, X * F1], F16)
        rth = sb("router_hi", [P, 2 * X], F16)
        rtl = sb("router_lo", [P, 2 * X], F16)
        b2h = sb("b2_hi", [X, 2, D], F16)
        hh = sb("hidden_hi", [P, 2, 512], F16)
        hl = sb("hidden_lo", [P, 2, 512], F16)
        h32 = sb("hidden", [P, 2, 512])
        yg = sb("expert_out", [P, 2, 512])
        lg = sb("logits", [P, T, X])
        ls = sb("logits_shifted", [P, T, X])
        ex = sb("exp_logits", [P, T, X])
        m8 = sb("sorted8", [P, T, 8])
        i8 = sb("sorted8_idx", [P, T, 8], U32)
        oh = sb("chosen", [P, T, X])
        oh2 = sb("chosen2", [P, T, X])
        gt = sb("expert_gate", [P, T, X])
        zs = sb("denom", [P, T])
        g1 = sb("gate1", [P, T])
        oh16 = sb("chosen16", [P, T, X], F16)
        before16 = sb("before16", [P, P], F16)
        ones16 = sb("ones16", [P, P], F16)
        ident16 = sb("ident16", [P, P], F16)
        cmp = sb("count_over", [P, X, 8])
        ntile = sb("tiles_of", [P, X])
        bas8 = sb("base_terms", [P, X, X])
        base = sb("base", [P, X])
        pt8 = sb("pos_terms", [P, T, X])
        pos = sb("pos", [P, T])
        send = sb("slots_end", [1, X])
        tcmp = sb("tile_over", [1, TS, X])
        tex = sb("tile_expert", [1, TS])
        texi = sb("tile_expert_int", [1, TS], I32)
        diag = sb("pos_diag", [P, T, P], F16)
        posr = sb("pos_row", [P, B * N], F16)
        iotas = sb("slot_row", [P, S], F16)
        slotc = sb("slot_col", [P, TS])
        ohT = sb("chosenT", [X, T * P], F16)
        zh = sb("z_hi", [P, T, D], F16)
        zl = sb("z_lo", [P, T, D], F16)
        G = sb("gather_onehot", [P, 2, T, GT * P], F16)
        zsh = sb("sorted_hi", [P, 2, GT * P], F16)
        zsl = sb("sorted_lo", [P, 2, GT * P], F16)
        Q = sb("return_onehot", [P, 2, T * P], F16)
        yhl = sb("sorted_out", [P, 2, 2, D], F16)

        made = {}

        def s(name):
            if name not in made:
                made[name] = ctx.enter_context(nc.semaphore(name))
            return made[name]

        block = ctx.enter_context(nc.Block())

        def tok(a, b):
            return a[b].rearrange("(p k) d -> p k d", k=K)

        def half(t, b):
            return t[:, b * K:(b + 1) * K]

        def bc(a, shape):
            return a.unsqueeze(len(a.shape)).to_broadcast(shape)

        UW = X * P // 2
        W1S = 8
        w0f, w0hf, w0lf = (t[:, :, :].rearrange("p a n -> p (a n)") for t in (w0, w0h, w0l))
        w1f, w1hf, w1lf = (t[:, :, :].rearrange("p a n -> p (a n)") for t in (w1, w1h, w1l))
        W1W = 2 * X * F1 // W1S

        @block.sync
        def _(sp):
            sp.dma_start(early[:, 0:eo["wk0"][0]], A["early"][:, 0:eo["wk0"][0]]).then_inc(s("early_in"), 16)
            sp.dma_start(half(x, 0), tok(A["x"], 0)).then_inc(s("x_in0"), 16)
            sp.dma_start(early[:, eo["wk0"][0]:], A["early"][:, eo["wk0"][0]:]).then_inc(s("weights0_in"), 16)
            sp.dma_start(half(x, 1), tok(A["x"], 1)).then_inc(s("x_in1"), 16)
            sp.dma_start(w0[:, :, :], A["w0"]).then_inc(s("w0_in"), 16)
            sp.dma_start(lay1[:, :, :], A["attn1"]).then_inc(s("attn1_in"), 16)
            sp.dma_start(late[:, :], A["late"]).then_inc(s("late_in"), 16)
            for i in range(2):
                sp.dma_start(w1[:, i, :], A["w1"][:, i, :]).then_inc(s(f"w1_in{i}"), 16)
            for b in range(B):
                sp.wait_ge(s("x4"), b + 1)
                sp.dma_start(tok(out, b), half(x, b)).then_inc(s("stored"), 16)
            sp.wait_ge(s("stored"), 16 * B)

        @block.gpsimd
        def _(pool):
            pool.memset(nhalf[:, :], -0.5).then_inc(s("nhalf"), 1)
            pool.memset(onesf[:, :], 1.0)
            pool.memset(ones16[:, :], 1.0).then_inc(s("ones"), 1)
            pool.wait_ge(s("nhalf"), 1)
            pool.wait_ge(s("cvar"), 1)
            pool.tensor_tensor(crs[:, :], cva[:, :], nhalf[0:J, 0:1], ALU.pow).then_inc(s("crstd"), 1)

            def rstd(i, b):
                pool.wait_ge(s("var"), i * B + b + 1)
                pool.tensor_tensor(half(rs, b), half(va, b), half(nhalf, b), ALU.pow).then_inc(s("rstd"), 1)

            def add_bias(i, b):
                if i == 0:
                    pool.wait_ge(s("bias_gated"), 1)
                pool.tensor_tensor(half(xb, b), half(x, b), bog[:, i].unsqueeze(1).to_broadcast([P, K, D]), ALU.add).then_inc(s("xb"), 1)

            def low_part(dst, src, hi, a, n):
                return pool.tensor_tensor(dst[:, a:a + n], src[:, a:a + n], hi[:, a:a + n], ALU.subtract)

            rstd(0, 0)
            rstd(0, 1)
            add_bias(0, 0)
            add_bias(0, 1)
            for i in range(4):
                pool.wait_ge(s("w0_hi"), i + 1)
                low_part(w0lf, w0f, w0hf, i * UW, UW).then_inc(s("w0_lo"), 1)
            pool.iota(iotas[:, :], [[1, S]], base=0, channel_multiplier=0, allow_small_or_imprecise_dtypes=True)
            pool.iota(slotc[:, :], [[P, TS]], base=0, channel_multiplier=1, allow_small_or_imprecise_dtypes=True).then_inc(s("iotas"), 1)
            rstd(1, 0)
            rstd(1, 1)

            def collect(u):
                b = u // X
                pool.wait_ge(s("y_gated"), u + 1)
                if u:
                    pool.wait_ge(s("x2"), u)
                pool.tensor_tensor(half(x, b), half(x, b), yg[:, u % 2, :].rearrange("p (k d) -> p k d", k=K), ALU.add).then_inc(s("x2"), 1)

            for u in range(X):
                collect(u)
            for u in range(X, 2 * X):
                collect(u)
                if u == X + 2:
                    rstd(2, 0)
                    add_bias(1, 0)
            rstd(2, 1)
            add_bias(1, 1)
            for i in range(W1S):
                pool.wait_ge(s("w1_hi"), i + 1)
                low_part(w1lf, w1f, w1hf, i * W1W, W1W).then_inc(s("w1_lo"), 1)
                if i == 3:
                    rstd(3, 0)
                if i == 5:
                    rstd(3, 1)

        @block.scalar
        def _(act):
            a = nc.scalar
            act.wait_ge(s("early_in"), 16)
            a.activation(tg[:, :], E("gates"), ACT.Tanh).then_inc(s("tanh"), 1)

            def zT_hi(i, b):
                act.wait_ge(s("zT_ps"), i * B + b + 1)
                a.copy(zTh[:, b, :], bank[b][:, :]).then_inc(s("zT_hi"), 1)

            zT_hi(0, 0)
            zT_hi(0, 1)
            act.wait_ge(s("w0_in"), 16)
            for i in range(4):
                a.copy(w0hf[:, i * UW:(i + 1) * UW], w0f[:, i * UW:(i + 1) * UW]).then_inc(s("w0_hi"), 1)
                if i < 2:
                    act.wait_ge(s("shift0"), i + 1)
                    a.activation(pr[:, i, 0:P], sd[:, i, 0:P], ACT.Exp, scale=SC0).then_inc(s("exp0"), 1)
            for b in range(B):
                act.wait_ge(s("pT0_ps"), b + 1)
                a.copy(pTh[:, b, 0:P], bank[2 + b][:, P:2 * P]).then_inc(s("pT0_hi"), 1)
            zT_hi(1, 0)

            def lexp(i, b):
                act.wait_ge(s("lshift"), i * B + b + 1)
                a.activation(half(ex, b), half(ls, b), ACT.Exp).then_inc(s("lexp"), 1)

            lexp(0, 0)

            def hidden0(u):
                act.wait_ge(s("h_ps"), u + 1)
                if u >= 2:
                    act.wait_ge(s("y_ps"), u - 1)
                a.activation(hh[:, u % 2, :], bank[2 + u % 2][:, :], ACT.Relu).then_inc(s("h_hi"), 1)

            done = [0]

            def w1_hi():
                i = done[0]
                done[0] += 1
                if i % 4 == 0:
                    act.wait_ge(s(f"w1_in{i // 4}"), 16)
                a.copy(w1hf[:, i * W1W:(i + 1) * W1W], w1f[:, i * W1W:(i + 1) * W1W]).then_inc(s("w1_hi"), 1)

            for u in range(2 * X):
                hidden0(u)
                if u == 1:
                    zT_hi(1, 1)
                if u == 3:
                    lexp(0, 1)
                if u in (4, 6, 8, 14):
                    w1_hi()
                if u == X + 4:
                    zT_hi(2, 0)
            for q in range(T // 2):
                act.wait_ge(s("shift1"), q + 1)
                a.activation(pr[:, q % 2, :], sd[:, q % 2, :], ACT.Exp, scale=SC1).then_inc(s("exp1"), 1)
                if q == 0:
                    zT_hi(2, 1)
                w1_hi()
                act.wait_ge(s("pT1_ps"), q + 1)
                if q >= 2:
                    act.wait_ge(s("o1_ps"), q - 1)
                a.copy(pTh[:, q % 2, :], bank[4 + q % 2][:, :]).then_inc(s("pT1_hi"), 1)
            for b in range(B):
                zT_hi(3, b)
            for b in range(B):
                a.copy(half(zh, b), half(z, b)).then_inc(s("z_hi"), 1)
            lexp(1, 0)
            lexp(1, 1)

            def sorted_hi(g):
                w = min(GT, TS - g * GT) * P
                act.wait_ge(s("gather_ps"), g + 1)
                if g >= 2:
                    act.wait_ge(s("h1_ps"), GT * (g - 1))
                a.copy(zsh[:, g % 2, 0:w], bank[4 + g % 2][:, 0:w]).then_inc(s("sorted_hi"), 1)

            sorted_hi(0)
            for t in range(TS):
                act.wait_ge(s("h1"), t + 1)
                if t >= 2:
                    act.wait_ge(s("y1_ps"), t - 1)
                a.activation(hh[:, t % 2, :], h32[:, t % 2, :], ACT.Relu).then_inc(s("h1_hi"), 1)
                if t % GT == 0 and t // GT + 1 < NG:
                    sorted_hi(t // GT + 1)
                act.wait_ge(s("y1_ps"), t + 1)
                if t >= 2:
                    act.wait_ge(s("returned"), t - 1)
                a.copy(yhl[:, t % 2, 0, :], bank[7][:, 0:D]).then_inc(s("y1_hi"), 1)

        @block.tensor
        def _(pe):
            mm, tr = nc.tensor.matmul, nc.tensor.transpose

            def mm3(out_ap, sh, sl, mh, ml, start=True, stop=True):
                mm(out_ap, sh, mh, start=start, stop=False, skip_group_check=True)
                mm(out_ap, sh, ml, start=False, stop=False, skip_group_check=True)
                return mm(out_ap, sl, mh, start=False, stop=stop, skip_group_check=True)

            pe.wait_ge(s("early_in"), 16)
            pe.wait_ge(s("cz"), 1)
            tr(bank[6][0:DC, 0:J], cz[:, :], ident[0:J, 0:J]).then_inc(s("ctx_tr"), 1)
            pe.wait_ge(s("ctx_T"), 1)
            pe.wait_ge(s("weights0_in"), 16)
            mm(bank[7][:, 0:J], E("wk0", DC), c2T[:, :], start=True, stop=True)
            mm(bank[7][:, J:2 * J], E("wv0", DC), c2T[:, :], start=True, stop=True).then_inc(s("kv0_ps"), 1)

            def transpose_z(i, b):
                pe.wait_ge(s("z"), i * B + b + 1)
                for k in range(K):
                    last = tr(bank[b][:, k * P:(k + 1) * P], z[:, b * K + k, :], ident[:, :])
                last.then_inc(s("zT_ps"), 1)

            transpose_z(0, 0)
            pe.wait_ge(s("kv0"), 1)
            mm(bank[5][:, 0:J], E("wq0T"), kT0[:, :], start=True, stop=True).then_inc(s("kq0_ps"), 1)
            for b in range(B):
                last = mm(bank[6][:, b * D:(b + 1) * D], vT0[:, b], E("wo0"), start=True, stop=True)
            last.then_inc(s("vo0_ps"), 1)
            transpose_z(0, 1)
            pe.wait_ge(s("kq0"), 1)
            vec = E("vecs")
            mm(bank[7][0:1, 256:256 + J], vec[:, 1:2], kq0[:, :], start=True, stop=False)
            mm(bank[7][0:1, 256:256 + J], vec[:, 2:3], kT0[:, :], start=False, stop=True).then_inc(s("c0_ps"), 1)
            pe.wait_ge(s("c0"), 1)
            for b in range(B):
                pe.wait_ge(s("zT_lo"), b + 1)
                mm(bank[2 + b][:, 0:P], onesf[:, :], c0h[0:1, b], start=True, stop=True, skip_group_check=True)
                mm(bank[2 + b][:, 0:P], onesf[:, :], c0l[0:1, b], start=False, stop=True, skip_group_check=True)
                for k in range(K):
                    last = mm3(bank[2 + b][:, k * NC:(k + 1) * NC], zTh[:, b, k * P:(k + 1) * P], zTl[:, b, k * P:(k + 1) * P],
                               kq0h[:, b * NC:(b + 1) * NC], kq0l[:, b * NC:(b + 1) * NC], start=False)
                last.then_inc(s("s0_ps"), 1)
            pe.wait_ge(s("attn1_in"), 16)
            for c in range(C1):
                mm(bank[4][:, c * J:(c + 1) * J], lay1[0:DC, 1, c * P:(c + 1) * P], E("ctxT", DC), start=True, stop=True)
            for c in range(C1):
                last = mm(bank[4][:, 256 + c * J:256 + (c + 1) * J], lay1[0:DC, 2, c * P:(c + 1) * P], E("ctxT", DC), start=True, stop=True)
            last.then_inc(s("kv1_ps"), 1)
            for b in range(B):
                pe.wait_ge(s("p0"), b + 1)
                tr(bank[2 + b][:, P:2 * P], pr[:, b, 0:P], ident[:, :]).then_inc(s("pT0_ps"), 1)
            pe.wait_ge(s("vo0"), 1)
            for b in range(B):
                pe.wait_ge(s("pT0_lo"), b + 1)
                mm3(bank[b][:, :], pTh[:, b, 0:P], pTl[:, b, 0:P], vo0h[:, b], vo0l[:, b]).then_inc(s("o0_ps"), 1)
            pe.wait_ge(s("kv1"), 1)
            for c in range(C1):
                last = mm(bank[5][:, c * P:(c + 1) * P], lay1[:, 0, c * P:(c + 1) * P], kb1[:, c], start=True, stop=True)
            last.then_inc(s("kq1_ps"), 1)
            for b in range(B):
                for c in range(C1):
                    r = 64 * (c % 2)
                    at = (b * 2 + c // 2) * D
                    last = mm(bank[4][r:r + 64, at:at + D], vb1[:, c, b], lay1[:, 3, c * P:(c + 1) * P], start=True, stop=True)
            last.then_inc(s("vo1_ps"), 1)

            def logits(i, b):
                pe.wait_ge(s("zT_lo"), i * B + b + 1)
                pe.wait_ge(s("router"), 1)
                for k in range(K):
                    at = (b * K + k) * X
                    last = mm3(bank[6 + b][:, at:at + X], zTh[:, b, k * P:(k + 1) * P], zTl[:, b, k * P:(k + 1) * P],
                               rth[:, i // 2 * X:(i // 2 + 1) * X], rtl[:, i // 2 * X:(i // 2 + 1) * X])
                last.then_inc(s("lg_ps"), 1)

            transpose_z(1, 0)
            pe.wait_ge(s("vo1"), 1)
            logits(1, 0)
            pe.wait_ge(s("w0_lo"), 4)

            def up0(u):
                e, b = u % X, u // X
                if u >= 2:
                    pe.wait_ge(s("h_lo"), u - 1)
                mm3(bank[2 + u % 2][:, :], w0h[:, 0, e * P:(e + 1) * P], w0l[:, 0, e * P:(e + 1) * P], zTh[:, b, :], zTl[:, b, :]).then_inc(s("h_ps"), 1)

            def down0(u):
                e, b = u % X, u // X
                pe.wait_ge(s("h_lo"), u + 1)
                if u >= 2:
                    pe.wait_ge(s("y_gated"), u - 1)
                for k in range(K):
                    last = mm3(bank[4 + u % 2][:, k * D:(k + 1) * D], hh[:, u % 2, k * P:(k + 1) * P], hl[:, u % 2, k * P:(k + 1) * P],
                               w0h[:, 1, e * P:(e + 1) * P], w0l[:, 1, e * P:(e + 1) * P])
                last.then_inc(s("y_ps"), 1)

            up0(0)
            for u in range(2 * X):
                if u + 1 < 2 * X:
                    up0(u + 1)
                down0(u)
                if u == 0:
                    transpose_z(1, 1)
                if u == 1:
                    logits(1, 1)
                if u == X + 3:
                    transpose_z(2, 0)

            def scores1(q):
                b = q // 2
                if q >= 2:
                    pe.wait_ge(s("shift1"), q - 1)
                pe.wait_ge(s("zT_lo"), 2 * B + b + 1)
                for v in range(2):
                    k = (q % 2) * 2 + v
                    last = mm3(bank[2 + q % 2][:, v * 256:(v + 1) * 256], zTh[:, b, k * P:(k + 1) * P], zTl[:, b, k * P:(k + 1) * P], kq1h[:, b], kq1l[:, b])
                last.then_inc(s("s1_ps"), 1)

            def turn1(q):
                pe.wait_ge(s("p1"), q + 1)
                for v in range(4):
                    last = tr(bank[4 + q % 2][:, v * P:(v + 1) * P], pr[:, q % 2, v * P:(v + 1) * P], ident[:, :])
                last.then_inc(s("pT1_ps"), 1)

            def mix1(q):
                b = q // 2
                pe.wait_ge(s("pT1_lo"), q + 1)
                if q >= 2:
                    pe.wait_ge(s("x3"), q - 1)
                for v in range(2):
                    for g in range(2):
                        c = (v * 2 + g) * P
                        last = mm3(bank[6 + q % 2][:, v * D:(v + 1) * D], pTh[:, q % 2, c:c + P], pTl[:, q % 2, c:c + P],
                                   vo1h[:, b, g, :], vo1l[:, b, g, :], start=g == 0, stop=g == 1)
                last.then_inc(s("o1_ps"), 1)

            pe.wait_ge(s("y_gated"), 2 * X)
            scores1(0)
            scores1(1)
            turn1(0)
            transpose_z(2, 1)
            for q in range(T // 2):
                if q + 2 < T // 2:
                    scores1(q + 2)
                if q + 1 < T // 2:
                    turn1(q + 1)
                mix1(q)
            for b in range(B):
                transpose_z(3, b)
            for b in range(B):
                logits(3, b)
            rank = bank[7][:, 128:128 + (T + 1) * X]
            pe.wait_ge(s("chosen"), 1)
            mm(rank[:, 0:T * X], before16[:, :], oh16[:, :, :], start=True, stop=True, skip_group_check=True)
            for k in range(T):
                n = T - k
                last = mm(rank[:, (k + 1) * X:].rearrange("p (t e) -> p t e", e=X), ones16[:, :],
                          oh16[:, k, :].unsqueeze(1).to_broadcast([P, n, X]), start=False, stop=True, skip_group_check=True)
            last.then_inc(s("rank_ps"), 1)
            ohT_ps = bank[6][0:X, :].bitcast(F16)
            for k in range(T):
                last = tr(ohT_ps[:, k * P:(k + 1) * P], oh16[:, k, :], ident16[:, :])
            last.then_inc(s("chosenT_ps"), 1)

            def gather(g):
                w = min(GT, TS - g * GT) * P
                if g >= 2:
                    pe.wait_ge(s("sorted_lo"), g - 1)
                pe.wait_ge(s("z_lo"), B)
                for k in range(T):
                    pe.wait_ge(s("onehot"), g * T + k + 1)
                    mm(bank[4 + g % 2][:, 0:w], zh[:, k, :], G[:, g % 2, k, 0:w], start=k == 0, stop=False)
                    last = mm(bank[4 + g % 2][:, 0:w], zl[:, k, :], G[:, g % 2, k, 0:w], start=False, stop=k == T - 1)
                last.then_inc(s("gather_ps"), 1)

            gather(0)
            for b in range(B):
                pe.wait_ge(s("diag"), b + 1)
                for k in range(K):
                    last = mm(bank[b][:, k * P:(k + 1) * P], ones16[:, :], diag[:, b * K + k, :], start=True, stop=True)
                last.then_inc(s("pos_ps"), 1)
            pe.wait_ge(s("chosenT"), 1)
            pe.wait_ge(s("pos_row"), B)

            def ret(t):
                return bank[t // 2][:, (t % 2) * 256:(t % 2) * 256 + 2 * D]

            for t in range(T):
                mm(ret(t), ohT[:, t * P:(t + 1) * P], b2h[:, :, :], start=t % 2 == 0, stop=False, skip_group_check=True)
            pe.wait_ge(s("tile_expert"), 1)
            pe.wait_ge(s("w1_lo"), W1S)

            def up1(t):
                g, o = t // GT, t % GT * P
                e = nc.tensor.value_load(texi[0:1, t:t + 1], min_val=0, max_val=X - 1)
                pe.wait_ge(s("sorted_lo"), g + 1)
                if t >= 1:
                    pe.wait_ge(s("h1"), t)
                for c in range(M1):
                    at = bass.ds(e * F1 + c * P, P)
                    last = mm3(bank[6][:, c * P:(c + 1) * P], w1h[:, 0, at], w1l[:, 0, at], zsh[:, g % 2, o:o + P], zsl[:, g % 2, o:o + P])
                last.then_inc(s("h1_ps"), 1)
                return e

            def down1(t, e):
                pe.wait_ge(s("h1_lo"), t + 1)
                if t >= 1:
                    pe.wait_ge(s("y1_lo"), t)
                for c in range(M1):
                    at = bass.ds(e * F1 + c * P, P)
                    last = mm3(bank[7][:, 0:D], hh[:, t % 2, c * P:(c + 1) * P], hl[:, t % 2, c * P:(c + 1) * P],
                               w1h[:, 1, at], w1l[:, 1, at], start=c == 0, stop=c == M1 - 1)
                last.then_inc(s("y1_ps"), 1)

            def give_back(t):
                pe.wait_ge(s("y1_lo"), t + 1)
                pe.wait_ge(s("return_onehot"), t + 1)
                for k in range(T):
                    last = mm(ret(k), Q[:, t % 2, k * P:(k + 1) * P], yhl[:, t % 2], start=False, stop=t == TS - 1, skip_group_check=True)
                last.then_inc(s("returned"), 1)

            e = up1(0)
            for t in range(TS):
                if t % GT == 0 and t // GT + 1 < NG:
                    gather(t // GT + 1)
                if t + 1 < TS:
                    e_next = up1(t + 1)
                if t:
                    give_back(t - 1)
                down1(t, e)
                e = e_next
            give_back(TS - 1)

        @block.vector
        def _(dve):
            v = nc.vector
            step = [0]

            def link(ins):
                step[0] += 1
                ins.then_inc(s("dve_step"), 1)
                dve.wait_ge(s("dve_step"), step[0])

            def stats(i, b):
                for k in range(K):
                    last = v.bn_stats(st[:, b * K + k, :], x[:, b * K + k, :])
                link(last)
                for k in range(K):
                    last = v.bn_aggr(mv[:, b * K + k, :], st[:, b * K + k, :])
                link(last)
                if i == 0:
                    v.tensor_scalar(half(va, b), mv[:, b * K:(b + 1) * K, 1], 1.0 + EPS, EPS * EPS, ALU.mult, ALU.add).then_inc(s("var"), 1)
                else:
                    v.tensor_scalar(half(va, b), mv[:, b * K:(b + 1) * K, 1], EPS, None, ALU.add).then_inc(s("var"), 1)

            def apply(i, b):
                dve.wait_ge(s("rstd"), i * B + b + 1)
                for k in range(K):
                    t = b * K + k
                    last = v.tensor_scalar(z[:, t, :], x[:, t, :], mv[:, t, 0:1], rs[:, t:t + 1], ALU.subtract, ALU.mult)
                last.then_inc(s("z"), 1)

            def zT_lo(i, b):
                dve.wait_ge(s("zT_hi"), i * B + b + 1)
                v.tensor_tensor(zTl[:, b, :], bank[b][:, :], zTh[:, b, :], ALU.subtract).then_inc(s("zT_lo"), 1)

            def split(hi, lo, src):
                link(v.tensor_copy(hi, src))
                return v.tensor_tensor(lo, src, hi, ALU.subtract)

            dve.wait_ge(s("early_in"), 16)
            link(v.bn_stats(cst[:, :], E("ctx", J)))
            link(v.bn_aggr(cmv[:, :], cst[:, :]))
            v.tensor_scalar(cva[:, :], cmv[:, 1:2], EPS, None, ALU.add).then_inc(s("cvar"), 1)
            dve.wait_ge(s("crstd"), 1)
            v.tensor_scalar(cz[:, :], E("ctx", J), cmv[:, 0:1], crs[:, 0:1], ALU.subtract, ALU.mult).then_inc(s("cz"), 1)
            dve.wait_ge(s("x_in0"), 16)
            stats(0, 0)
            vec = E("vecs")
            dve.wait_ge(s("ctx_tr"), 1)
            v.tensor_scalar(c2T[:, :], bank[6][0:DC, 0:J], vec[0:DC, 5:6], vec[0:DC, 6:7], ALU.mult, ALU.add).then_inc(s("ctx_T"), 1)
            apply(0, 0)
            dve.wait_ge(s("x_in1"), 16)
            stats(0, 1)
            dve.wait_ge(s("kv0_ps"), 1)
            v.tensor_scalar(kT0[:, :], bank[7][:, 0:J], vec[:, 3:4], None, ALU.add)
            v.tensor_scalar(vT0[:, :, :, :], bank[7][:, J:2 * J].rearrange("p (b j) -> p b j", b=B).unsqueeze(2).to_broadcast([P, B, 4, NC]),
                            vec[:, 4:5], None, ALU.add).then_inc(s("kv0"), 1)
            apply(0, 1)
            dve.wait_ge(s("kq0_ps"), 1)
            v.tensor_copy(kq0[:, :], bank[5][:, 0:J]).then_inc(s("kq0"), 1)
            link(v.tensor_scalar(kq0g[:, :], bank[5][:, 0:J], vec[:, 0:1], None, ALU.mult))
            link(split(kq0h[:, :], kq0l[:, :], kq0g[:, :]))
            dve.wait_ge(s("tanh"), 1)
            link(v.tensor_scalar(mask4g[:, :], E("mask4"), tg[:, 0:1], None, ALU.mult))
            dve.wait_ge(s("c0_ps"), 1)
            link(v.tensor_copy(c0f[:, :], bank[7][0:1, 256:256 + J]))
            c0b = c0f[:, :].rearrange("p (b j) -> p b j", b=B).unsqueeze(2).to_broadcast([1, B, 4, NC])
            split(c0h[:, :, :, :], c0l[:, :, :, :], c0b).then_inc(s("c0"), 1)
            for b in range(B):
                zT_lo(0, b)
            dve.wait_ge(s("vo0_ps"), 1)
            for b in range(B):
                v.tensor_tensor(vo0[:, b], bank[6][:, b * D:(b + 1) * D].unsqueeze(1).to_broadcast([P, 4, D]),
                                bc(mask4g[:, :], [P, 4, D]), ALU.mult)
            for i in range(2):
                last = v.tensor_scalar(bog[:, i], E(f"bo{i}"), tg[:, i:i + 1], None, ALU.mult)
            last.then_inc(s("bias_gated"), 1)

            def softmax(Sc, q, Gr, w, shift, expd, done, count, between=None):
                sq, pq = (t[:, q, 0:Gr * w].rearrange("p (g w) -> p g w", g=Gr) for t in (sd, pr))
                m, u, r = mx[:, q, 0:Gr], sm[:, q, 0:Gr], ri[:, q, 0:Gr]
                link(v.tensor_reduce(m, Sc, AX.X, ALU.max))
                v.tensor_tensor(sq, Sc, bc(m, [P, Gr, w]), ALU.subtract).then_inc(s(shift), 1)
                if between:
                    between()
                dve.wait_ge(s(expd), count)
                link(v.tensor_reduce(u, pq, AX.X, ALU.add))
                link(v.reciprocal(r, u))
                v.tensor_tensor(pq, pq, bc(r, [P, Gr, w]), ALU.mult).then_inc(s(done), 1)

            def split_vo0(b):
                split(vo0h[:, b], vo0l[:, b], vo0[:, b]).then_inc(s("vo0"), 1)

            for b in range(B):
                dve.wait_ge(s("s0_ps"), b + 1)
                softmax(bank[2 + b][:, 0:P].rearrange("p (k j) -> p k j", k=K), b, K, NC, "shift0", "exp0", "p0", b + 1,
                        lambda: link(split(vo0h[:, b], vo0l[:, b], vo0[:, b])))
            v.tensor_copy(mask4g[:, 0:1], mask4g[:, 0:1]).then_inc(s("vo0"), 1)
            dve.wait_ge(s("kv1_ps"), 1)
            for hd in range(2):
                v.tensor_scalar(kb1[:, :, hd, :], bank[4][:, 0:256].rearrange("p (c j) -> p c j", c=C1), E("mask2")[:, hd:hd + 1], None, ALU.mult)
            for hd in range(2):
                last = v.tensor_scalar(vb1[:, :, :, hd, :], bank[4][:, 256:512].rearrange("p (c b j) -> p c b j", c=C1, b=B), E("mask2")[:, hd:hd + 1], None, ALU.mult)
            last.then_inc(s("kv1"), 1)
            for b in range(B):
                dve.wait_ge(s("pT0_hi"), b + 1)
                v.tensor_tensor(pTl[:, b, 0:P], bank[2 + b][:, P:2 * P], pTh[:, b, 0:P], ALU.subtract).then_inc(s("pT0_lo"), 1)

            def first_out(b):
                dve.wait_ge(s("o0_ps"), b + 1)
                dve.wait_ge(s("xb"), b + 1)
                link(v.tensor_tensor(half(x, b), bank[b][:, :].rearrange("p (k d) -> p k d", k=K), half(xb, b), ALU.add))
                stats(1, b)

            first_out(0)
            dve.wait_ge(s("late_in"), 16)
            split(rth[:, :], rtl[:, :], late[:, 0:2 * X]).then_inc(s("router"), 1)
            first_out(1)
            apply(1, 0)
            dve.wait_ge(s("kq1_ps"), 1)
            for b in range(B):
                v.tensor_copy(kq1[:, b].rearrange("p (h j) -> p h j", h=H1), bank[5][:, :].rearrange("p (h b j) -> p h b j", h=H1, b=B)[:, :, b, :])
            dve.wait_ge(s("vo1_ps"), 1)
            v.tensor_scalar(vo1[:, :, :, :].rearrange("p b g d -> p (b g d)"), bank[4][:, :], tg[:, 1:2], None, ALU.mult).then_inc(s("vo1"), 1)
            zT_lo(1, 0)
            apply(1, 1)

            def gate(i, b, kind):
                full = [P, K, X]
                dve.wait_ge(s("lg_ps"), i * B + b + 1)
                ps = bank[6 + b][:, b * K * X:(b + 1) * K * X].rearrange("p (t e) -> p t e", t=K)
                if i == 0:
                    link(v.tensor_copy(half(lg, b), ps))
                else:
                    link(v.tensor_tensor(half(lg, b), ps, Lt("b_gate").unsqueeze(1).to_broadcast(full), ALU.add))
                for k in range(K):
                    last = v.max(m8[:, b * K + k, :], lg[:, b * K + k, :])
                link(last)
                v.tensor_tensor(half(ls, b), half(lg, b), bc(m8[:, b * K:(b + 1) * K, 0], full), ALU.subtract).then_inc(s("lshift"), 1)
                for k in range(K):
                    last = v.max_index(i8[:, b * K + k, :], m8[:, b * K + k, :], lg[:, b * K + k, :])
                link(last)
                which = Lt("iota8").unsqueeze(1).to_broadcast(full)
                last = v.tensor_tensor(half(oh, b), which, bc(i8[:, b * K:(b + 1) * K, 0], full), ALU.is_equal)
                if i == 0:
                    link(v.tensor_tensor(half(oh2, b), which, bc(i8[:, b * K:(b + 1) * K, 1], full), ALU.is_equal))
                    link(v.tensor_tensor(half(oh, b), half(oh, b), half(oh2, b), ALU.add))
                else:
                    v.tensor_tensor(half(oh16, b), which, bc(i8[:, b * K:(b + 1) * K, 0], full), ALU.is_equal)

            def gate_values(i, b):
                full = [P, K, X]
                dve.wait_ge(s("lexp"), i * B + b + 1)
                link(v.tensor_reduce(half(zs, b), half(ex, b), AX.X, ALU.add))
                link(v.reciprocal(half(zs, b), half(zs, b)))
                link(v.tensor_scalar(half(zs, b), half(zs, b), tg[:, 2 + i:3 + i], None, ALU.mult))
                if i == 0:
                    link(v.tensor_tensor(half(gt, b), half(ex, b), half(oh, b), ALU.mult))
                    link(v.tensor_tensor(half(gt, b), half(gt, b), bc(half(zs, b), full), ALU.mult))

            gate(0, 0, 0)
            gate_values(0, 0)

            def lo0(u):
                dve.wait_ge(s("h_hi"), u + 1)
                v.scalar_tensor_tensor(hl[:, u % 2, :], bank[2 + u % 2][:, :], 0.0, hh[:, u % 2, :], ALU.max, ALU.subtract).then_inc(s("h_lo"), 1)

            def gated(u):
                e, b = u % X, u // X
                dve.wait_ge(s("y_ps"), u + 1)
                if u >= 2:
                    dve.wait_ge(s("x2"), u - 1)
                v.tensor_tensor(yg[:, u % 2, :].rearrange("p (k d) -> p k d", k=K), bank[4 + u % 2][:, :].rearrange("p (k d) -> p k d", k=K),
                                bc(gt[:, b * K:(b + 1) * K, e], [P, K, D]), ALU.mult).then_inc(s("y_gated"), 1)

            lo0(0)
            for u in range(2 * X):
                if u + 1 < 2 * X:
                    lo0(u + 1)
                if u == 1:
                    zT_lo(1, 1)
                if u == 2:
                    gate(0, 1, 0)
                    gate_values(0, 1)
                if u == 4:
                    link(split(kq1h[:, :, :], kq1l[:, :, :], kq1[:, :, :]))
                if u == 5:
                    link(split(vo1h[:, :, :, :], vo1l[:, :, :, :], vo1[:, :, :, :]))
                if u == 6:
                    v.tensor_copy(before16[:, :], Lt("before"))
                    v.tensor_copy(ident16[:, :], ident)
                    link(split(b2h[:, 0, :], b2h[:, 1, :], Lt("b2", X)))
                gated(u)
                if u == X + 1:
                    dve.wait_ge(s("x2"), X)
                    stats(2, 0)
                if u == X + 3:
                    apply(2, 0)
                if u == X + 4:
                    zT_lo(2, 0)
            dve.wait_ge(s("x2"), 2 * X)
            stats(2, 1)

            def lo1(q):
                dve.wait_ge(s("pT1_hi"), q + 1)
                v.tensor_tensor(pTl[:, q % 2, :], bank[4 + q % 2][:, :], pTh[:, q % 2, :], ALU.subtract).then_inc(s("pT1_lo"), 1)

            def out1(q):
                dve.wait_ge(s("o1_ps"), q + 1)
                dve.wait_ge(s("xb"), B + q // 2 + 1)
                v.tensor_tensor(x[:, 2 * q:2 * q + 2, :], bank[6 + q % 2][:, 0:2 * D].rearrange("p (u d) -> p u d", u=2),
                                xb[:, 2 * q:2 * q + 2, :], ALU.add).then_inc(s("x3"), 1)

            for q in range(T // 2):
                dve.wait_ge(s("s1_ps"), q + 1)
                if q >= 2:
                    dve.wait_ge(s("pT1_ps"), q - 1)
                    out1(q - 2)

                def between():
                    if q == 0:
                        apply(2, 1)
                    if q == 1:
                        zT_lo(2, 1)
                    if q:
                        lo1(q - 1)
                    if q == 3:
                        dve.wait_ge(s("x3"), 2)
                        stats(3, 0)
                softmax(bank[2 + q % 2][:, :].rearrange("p (g j) -> p g j", j=NC), q % 2, 16, NC, "shift1", "exp1", "p1", q + 1, between)
            out1(T // 2 - 2)
            lo1(T // 2 - 1)
            apply(3, 0)
            out1(T // 2 - 1)
            dve.wait_ge(s("x3"), T // 2)
            stats(3, 1)
            zT_lo(3, 0)
            apply(3, 1)
            zT_lo(3, 1)
            gate(1, 0, 1)
            gate(1, 1, 1)
            v.tensor_copy(zs[:, 0:1], zs[:, 0:1]).then_inc(s("chosen"), 1)
            for b in range(B):
                dve.wait_ge(s("z_hi"), b + 1)
                v.tensor_tensor(half(zl, b), half(z, b), half(zh, b), ALU.subtract).then_inc(s("z_lo"), 1)
            dve.wait_ge(s("rank_ps"), 1)
            rank = bank[7][:, 128:128 + (T + 1) * X].rearrange("p (t e) -> p t e", e=X)
            link(v.tensor_tensor(cmp[:, :, :], bc(rank[:, T, :], [P, X, 8]), Lt("thresholds").rearrange("p (e j) -> p e j", e=X), ALU.is_gt))
            link(v.tensor_reduce(ntile[:, :], cmp[:, :, :], AX.X, ALU.add))
            link(v.tensor_tensor(bas8[:, :, :], ntile[:, :].unsqueeze(1).to_broadcast([P, X, X]), Lt("before8").rearrange("p (e j) -> p e j", e=X), ALU.mult))
            link(v.tensor_reduce(base[:, :], bas8[:, :, :], AX.X, ALU.add))
            link(v.tensor_tensor(pt8[:, :, :], rank[:, 0:T, :], base[:, :].unsqueeze(1).to_broadcast([P, T, X]), ALU.add))
            link(v.tensor_tensor(pt8[:, :, :], pt8[:, :, :], oh[:, :, :], ALU.mult))
            link(v.tensor_reduce(pos[:, :], pt8[:, :, :], AX.X, ALU.add))
            dve.wait_ge(s("iotas"), 1)

            def onehots(g):
                w = min(GT, TS - g * GT) * P
                if g >= 2:
                    dve.wait_ge(s("gather_ps"), g - 1)
                for k in range(T):
                    v.tensor_scalar(G[:, g % 2, k, 0:w], iotas[:, g * GT * P:g * GT * P + w], pos[:, k:k + 1], None, ALU.is_equal).then_inc(s("onehot"), 1)

            onehots(0)
            for b in range(B):
                for k in range(K):
                    last = v.tensor_scalar(diag[:, b * K + k, :], ident16[:, :], pos[:, b * K + k:b * K + k + 1], None, ALU.mult)
                last.then_inc(s("diag"), 1)
            link(v.scalar_tensor_tensor(send[:, :], ntile[0:1, :], float(P), base[0:1, :], ALU.mult, ALU.add))
            link(v.tensor_tensor(tcmp[:, :, :], send[:, :].unsqueeze(1).to_broadcast([1, TS, X]), Lt("tile_starts", 1).rearrange("p (t e) -> p t e", t=TS), ALU.is_le))
            link(v.tensor_reduce(tex[:, :], tcmp[:, :, :], AX.X, ALU.add))
            v.tensor_scalar(texi[:, :], tex[:, :], float(X - 1), None, ALU.min).then_inc(s("tile_expert"), 1)
            dve.wait_ge(s("chosenT_ps"), 1)
            v.tensor_copy(ohT[:, :], bank[6][0:X, :].bitcast(F16)).then_inc(s("chosenT"), 1)
            for b in range(B):
                dve.wait_ge(s("pos_ps"), b + 1)
                v.tensor_copy(posr[:, b * N:(b + 1) * N], bank[b][:, :]).then_inc(s("pos_row"), 1)

            def sorted_lo(g):
                w = min(GT, TS - g * GT) * P
                dve.wait_ge(s("sorted_hi"), g + 1)
                v.tensor_tensor(zsl[:, g % 2, 0:w], bank[4 + g % 2][:, 0:w], zsh[:, g % 2, 0:w], ALU.subtract).then_inc(s("sorted_lo"), 1)

            def return_onehot(t):
                if t >= 2:
                    dve.wait_ge(s("returned"), t - 1)
                v.tensor_scalar(Q[:, t % 2, :], posr[:, :], slotc[:, t:t + 1], None, ALU.is_equal).then_inc(s("return_onehot"), 1)

            sorted_lo(0)
            onehots(1)
            gate_values(1, 0)
            gate_values(1, 1)
            dve.wait_ge(s("tile_expert"), 1)
            dve.wait_ge(s("pos_row"), B)
            for t in range(TS):
                e = nc.vector.value_load(texi[0:1, t:t + 1], min_val=0, max_val=X - 1)
                dve.wait_ge(s("h1_ps"), t + 1)
                v.tensor_tensor(h32[:, t % 2, :].rearrange("p (c n) -> p c n", c=M1), bank[6][:, :].rearrange("p (c n) -> p c n", c=M1),
                                bc(Lt("b1")[:, bass.ds(e * M1, M1)], [P, M1, P]), ALU.add).then_inc(s("h1"), 1)
                if t:
                    dve.wait_ge(s("y1_hi"), t)
                    v.tensor_tensor(yhl[:, (t - 1) % 2, 1, :], bank[7][:, 0:D], yhl[:, (t - 1) % 2, 0, :], ALU.subtract).then_inc(s("y1_lo"), 1)
                dve.wait_ge(s("h1_hi"), t + 1)
                v.scalar_tensor_tensor(hl[:, t % 2, :], h32[:, t % 2, :], 0.0, hh[:, t % 2, :], ALU.max, ALU.subtract).then_inc(s("h1_lo"), 1)
                return_onehot(t)
                if t % GT == 0 and t // GT + 1 < NG:
                    sorted_lo(t // GT + 1)
                if t % GT == 1 and t // GT + 2 < NG:
                    onehots(t // GT + 2)
            dve.wait_ge(s("y1_hi"), TS)
            v.tensor_tensor(yhl[:, (TS - 1) % 2, 1, :], bank[7][:, 0:D], yhl[:, (TS - 1) % 2, 0, :], ALU.subtract).then_inc(s("y1_lo"), 1)
            dve.wait_ge(s("returned"), TS)
            for b in range(B):
                for part in range(2):
                    for k in range(K):
                        t = b * K + k
                        at = (t % 2) * 256 + part * D
                        last = v.scalar_tensor_tensor(x[:, t, :], bank[t // 2][:, at:at + D], zs[:, t:t + 1], x[:, t, :], ALU.mult, ALU.add)
                    if part == 0:
                        link(last)
                last.then_inc(s("x4"), 1)


_OUT = ((2, 512, 128), "float32")


def kernel(**inputs):
    import numpy as np
    import concourse.bacc as bacc
    from concourse import mybir
    from concourse.bass_utils import run_bass_kernel_spmd

    a = {k: np.asarray(v) for k, v in inputs.items()}
    X, M = 8, 4

    def table(columns, parts):
        at, width = offsets(columns)
        out = np.zeros((P, width), np.float32)
        for name, part in parts.items():
            lo, hi = at[name]
            part = np.asarray(part)
            out[0:part.shape[0], lo:hi] = part.reshape(part.shape[0], hi - lo)
        return out

    def rows(v, n=P):
        return np.broadcast_to(v.reshape(1, -1), (n, v.size))

    vecs = np.zeros((P, 7), np.float32)
    for i, name in enumerate(("ln1_g", "ln1_b", "bq", "bk", "bv", "ln2_g", "ln2_b")):
        v = a["L0_xattn_" + name]
        vecs[0:v.size, i] = v
    ctx = a["ctx_768"].reshape(64, 96)
    p = np.arange(P)
    sent = {
        "x": a["x"],
        "early": table(EARLY, {
            "ident": np.eye(P, dtype=np.float32), "ctx": ctx, "ctxT": ctx.T,
            "gates": rows(np.concatenate([a["g_xattn"], a["g_ffn"]])), "vecs": vecs,
            "mask4": p[:, None] // 32 == np.arange(4), "mask2": p[:, None] // 64 == np.arange(2),
            "wk0": a["L0_xattn_Wk"], "wv0": a["L0_xattn_Wv"], "wq0T": a["L0_xattn_Wq"].T, "wo0": a["L0_xattn_Wo"],
            "bo0": rows(a["L0_xattn_bo"]), "bo1": rows(a["L1_xattn_bo"]),
        }),
        "late": table(LATE, {
            "routerT": a["L0_ffn_router_w"].T, "w_gate": a["L1_ffn_w_gate"], "b_gate": rows(a["L1_ffn_b_gate"]),
            "b1": a["L1_ffn_b1"].reshape(X * M, P).T, "b2": a["L1_ffn_b2"],
            "before": p[:, None] < p[None, :], "iota8": rows(np.arange(X)),
            "before8": rows(P * (np.arange(X)[None, :] < np.arange(X)[:, None])),
            "thresholds": rows(np.broadcast_to(P * np.arange(8), (X, 8))),
            "tile_starts": rows(np.repeat(P * np.arange(15), X)),
        }),
        "w0": np.stack([a["L0_ffn_w1"].transpose(1, 0, 2).reshape(P, -1), a["L0_ffn_w2"].transpose(1, 0, 2).reshape(P, -1)], 1),
        "attn1": np.zeros((P, 4, 512), np.float32),
        "w1": np.stack([a["L1_ffn_W1"].transpose(1, 0, 2).reshape(P, -1),
                        a["L1_ffn_W2"].reshape(X, M, P, P).transpose(2, 0, 1, 3).reshape(P, -1)], 1),
    }
    sent["attn1"][:, 0] = a["L1_xattn_Wq"].T.reshape(4, P, P).transpose(1, 0, 2).reshape(P, -1)
    sent["attn1"][0:96, 1] = a["L1_xattn_Wk"]
    sent["attn1"][0:96, 2] = a["L1_xattn_Wv"]
    sent["attn1"][:, 3] = a["L1_xattn_Wo"].reshape(4, P, P).transpose(1, 0, 2).reshape(P, -1)

    nc = bacc.Bacc("TRN2", target_bir_lowering=False, num_devices=1)
    arrays, args = {}, {}
    for name, value in sent.items():
        value = np.ascontiguousarray(value)
        arrays[f"in_{name}_dram"] = value
        args[name] = nc.dram_tensor(f"in_{name}_dram", value.shape, mybir.dt.from_np(value.dtype), kind="ExternalInput").ap()
    out = nc.dram_tensor("out_0_dram", _OUT[0], mybir.dt.from_np(np.dtype(_OUT[1])), kind="ExternalOutput").ap()
    gated_blocks_kernel(nc, args, out)
    r = run_bass_kernel_spmd(nc, [arrays], core_ids=[0])
    return r.results[0]["out_0_dram"]
```

```python
import concourse.bass as bass
from concourse import mybir
from contextlib import ExitStack

P = 128
EPS = 1e-05
HALF_RANGE = 2048

ALU = mybir.AluOpType
ACT = mybir.ActivationFunctionType
AX = mybir.AxisListType
F32 = mybir.dt.float32
F16 = mybir.dt.float16
I32 = mybir.dt.int32
U32 = mybir.dt.uint32

EARLY = (("ident", 128), ("ctx", 96), ("ctxT", 64), ("gates", 4), ("vecs", 7), ("mask4", 4), ("mask2", 2),
         ("wk0", 128), ("wv0", 128), ("wq0T", 128), ("wo0", 128), ("bo0", 128), ("bo1", 128))
LATE = (("routerT", 8), ("w_gate", 8), ("b_gate", 8), ("before", 128), ("iota8", 8),
        ("before8", 64), ("thresholds", 64), ("tile_starts", 88), ("row_expert", 1))


def offsets(table):
    at, out = 0, {}
    for name, width in table:
        out[name] = (at, at + width)
        at += width
    return out, at


def gated_blocks_kernel(nc, A, out):
    B, N, D = A["x"].shape
    NC, DC = 32, 96
    K = N // P
    T = B * K
    J = B * NC
    X = 8
    H1, HD = 8, 64
    C1 = H1 * HD // P
    F1 = 512
    M1 = F1 // P
    TS = K + X - 1
    S = TS * P
    GROUPS = ((0, 1), (1, 3), (3, 7), (7, 11))
    NG, GW = len(GROUPS), 4
    assert GROUPS[-1][1] == TS
    BR = 32 + X
    SC0, SC1 = float(D) ** -0.5, float(HD) ** -0.5
    assert S <= HALF_RANGE

    with ExitStack() as ctx:
        def sb(name, shape, dt=F32):
            return ctx.enter_context(nc.sbuf_tensor(name, shape, dt))

        bank = [ctx.enter_context(nc.psum_tensor(f"bank{i}", [P, 512], F32)) for i in range(8)]

        eo, ew = offsets(EARLY)
        lo, lw = offsets(LATE)
        early = sb("early", [P, ew])
        late = sb("late", [P, lw])

        def E(name, rows=P):
            a, b = eo[name]
            return early[0:rows, a:b]

        def Lt(name, rows=P):
            a, b = lo[name]
            return late[0:rows, a:b]

        ident = E("ident")
        x = sb("x_res", [P, T, D])
        z = sb("z", [P, T, D])
        zTh = sb("zT_hi", [P, B, N], F16)
        zTl = sb("zT_lo", [P, B, N], F16)
        st = sb("stats", [P, T, 6])
        mv = sb("mean_var", [P, T, 2])
        va = sb("var_eps", [P, T])
        rs = sb("rstd", [P, T])
        nhalf = sb("minus_half", [P, T])
        mask4g = sb("mask4g", [P, 4])
        ones_row = sb("ones_row", [1, P], F16)
        ones_row32 = sb("ones_row32", [1, P])
        tg = sb("tanh_gates", [P, 4])
        cz = sb("ctx_norm", [J, DC])
        cst = sb("ctx_stats", [J, 6])
        cmv = sb("ctx_mean_var", [J, 2])
        cva = sb("ctx_var_eps", [J, 1])
        crs = sb("ctx_rstd", [J, 1])
        c2T = sb("ctx_normT", [DC, J])
        kT0 = sb("kT0", [P, J])
        vT0 = sb("vT0", [P, B, 4, NC])
        kq0 = sb("kq0", [D, J])
        kq0h = sb("kq0_hi", [D, J], F16)
        kq0l = sb("kq0_lo", [D, J], F16)
        c0h = sb("score_bias_hi", [1, B, 4, NC], F16)
        c0l = sb("score_bias_lo", [1, B, 4, NC], F16)
        vo0h = sb("vo0_hi", [P, B, 4, D], F16)
        vo0l = sb("vo0_lo", [P, B, 4, D], F16)
        lay1 = sb("attn1_weights", [P, 4, 512])
        kb1 = sb("k_blocks", [P, C1, 2, J])
        vb1 = sb("v_blocks", [P, C1, B, 2, NC])
        kq1h = sb("kq1_hi", [D, B, H1 * NC], F16)
        kq1l = sb("kq1_lo", [D, B, H1 * NC], F16)
        vo1h = sb("vo1_hi", [P, B, 2, D], F16)
        vo1l = sb("vo1_lo", [P, B, 2, D], F16)
        sd = sb("scores_shifted", [P, 2, 512])
        pr = sb("probs", [P, 2, 512])
        pTh = sb("probsT_hi", [P, 2, 512], F16)
        pTl = sb("probsT_lo", [P, 2, 512], F16)
        mx = sb("row_max", [P, 2, 16])
        sm = sb("row_sum", [P, 2, 16])
        ri = sb("row_inv", [P, 2, 16])
        w0 = sb("w0", [P, 2, X * P])
        w0h = sb("w0_hi", [P, 2, X * P], F16)
        w0l = sb("w0_lo", [P, 2, X * P], F16)
        w1 = sb("w1", [P, 2, X * F1])
        w1s = sb("w1_split", [P, X, 2, 2, F1], F16)
        NW = 4
        wt = sb("tile_weights", [P, NW, 2, 2, F1], F16)
        rth = sb("router_hi", [P, 2 * X], F16)
        rtl = sb("router_lo", [P, 2 * X], F16)
        b12f = sb("b12", [BR, F1 + D])
        b12s = sb("b12_hi_lo", [BR, F1 + D], F16)
        sel = sb("tile_is_expert", [BR, B, TS], F16)
        hh = sb("hidden_hi", [P, 3, 512], F16)
        hl = sb("hidden_lo", [P, 3, 512], F16)
        yg = sb("expert_out", [P, 3, 512])
        lg = sb("logits", [P, T, X])
        ls = sb("logits_shifted", [P, T, X])
        ex = sb("exp_logits", [P, T, X])
        m8 = sb("sorted8", [P, T, 8])
        i8 = sb("sorted8_idx", [P, T, 8], U32)
        oh = sb("chosen", [P, T, X])
        oh2 = sb("chosen2", [P, T, X])
        gt = sb("expert_gate", [P, T, X])
        zs = sb("denom", [P, T])
        oh16 = sb("chosen16", [P, T, X], F16)
        before16 = sb("before16", [P, P], F16)
        ones16 = sb("ones16", [P, P], F16)
        ident16 = sb("ident16", [P, P], F16)
        cmp = sb("count_over", [P, X, 8])
        ntile = sb("tiles_of", [P, B, X])
        bas8 = sb("base_terms", [P, X, X])
        base = sb("base", [P, B, X])
        pt8 = sb("pos_terms", [P, K, X])
        pos = sb("pos", [P, T])
        send = sb("slots_end", [BR, X])
        tcmp = sb("tile_over", [BR, TS, X])
        tex = sb("tile_expert", [BR, TS])
        texi = sb("tile_expert_int", [1, B * TS], I32)
        diag = sb("pos_diag", [P, T, P], F16)
        posr = sb("pos_row", [P, B * N], F16)
        iotas = sb("slot_row", [P, S], F16)
        slotc = sb("slot_col", [P, TS])
        zh = sb("z_hi", [P, T, D], F16)
        zl = sb("z_lo", [P, T, D], F16)
        G = w1[:, :, :].rearrange("p a n -> p (a n)").bitcast(F16)[:, 0:T * S].rearrange("p (k s) -> p k s", k=T)
        zsh = sb("sorted_hi", [P, 2, GW * P], F16)
        zsl = sb("sorted_lo", [P, 2, GW * P], F16)
        Q = sb("return_onehot", [P, 2, N], F16)
        yT = sb("returned_T", [P, N])
        yhl = sb("sorted_out", [P, 2, 2, D], F16)

        made = {}

        def s(name):
            if name not in made:
                made[name] = ctx.enter_context(nc.semaphore(name))
            return made[name]

        block = ctx.enter_context(nc.Block())

        def tok(a, b):
            return a[b].rearrange("(p k) d -> p k d", k=K)

        def half(t, b):
            return t[:, b * K:(b + 1) * K]

        def bc(a, shape):
            return a.unsqueeze(len(a.shape)).to_broadcast(shape)

        W0S = 4
        UW = 2 * X * P // W0S
        W1S = 2 * X
        w0f, w0hf, w0lf = (t[:, :, :].rearrange("p a n -> p (a n)") for t in (w0, w0h, w0l))
        w1f = w1[:, :, :].rearrange("p a n -> p (a n)")

        def w1_part(i, part):
            return w1s[:, i % X, i // X, part, :]

        def on_pool(g, k):
            return k in ((), (), (2, 3), range(K))[g] if g < NG else g > NG

        def slots(g):
            return GROUPS[g % NG][0] * P, GROUPS[g % NG][1] * P

        GATHER = {0: (2, 0, 2), 1: (2, 2, 4), 3: (3, 0, 2), 4: (3, 2, 4), 9: (4, 0, 4), 10: (5, 0, 4),
                  11: (6, 0, 2), 12: (6, 2, 4), 14: (7, 0, 2), 15: (7, 2, 4)}
        SORTED = {2: 2, 5: 3, 10: 4, 11: 5, 13: 6, 16: 7}
        TILES = B * TS

        def group_end(g):
            return g // NG * TS + GROUPS[g % NG][1]

        group_of = [g for g in range(B * NG) for _ in range(*GROUPS[g % NG])]

        def gather_onehot(eng, g, k):
            a, b = slots(g)
            t = g // NG * K + k
            return eng.tensor_scalar(G[:, t, a:b], iotas[:, a:b], pos[:, t:t + 1], None, ALU.is_equal)

        def onehots_made(pool_side, g, k):
            return sum(on_pool(i, j) == pool_side for i in range(g + 1) for j in range(K) if (i, j) <= (g, k))

        h0_bank, y0_bank = (bank[2], bank[3], bank[6]), (bank[4], bank[5], bank[7])
        score_bank = (bank[0], bank[6], bank[3], bank[2])
        probs_bank = (bank[1], bank[7], bank[4], bank[5])
        out_bank = (bank[0], bank[2], bank[6], bank[1])
        logit_bank = {(1, 0): bank[0], (1, 1): bank[1], (3, 0): bank[0], (3, 1): bank[1]}
        END_PARTS = (((0, K),), ((0, K // 2), (K // 2, K)))
        h1_bank = (bank[3], bank[6])
        turned_bank = ((bank[0],), (bank[4], bank[5]))

        def y1_bank(t):
            return 2 if t >= TS and t % 2 else 7

        def gather_bank(g):
            return 5 if g % 2 and g != 3 else 4

        def rank_ps(b):
            return bank[b][:, 128:128 + (K + 1) * X]

        def out1_ps(q):
            return out_bank[q][:, 0:2 * D]

        def last_user(which, i):
            return next((j for j in range(i - 1, -1, -1) if which(j) == which(i)), None)

        W1_EARLY = 7
        ACT_MORE = (5, 7, 11)

        def gated_on_act(u):
            return u % 2 == 0 or u in ACT_MORE

        def gated_count(u):
            return sum(gated_on_act(i) == gated_on_act(u) for i in range(u + 1))

        @block.sync
        def _(sp):
            sp.dma_start(early[:, 0:eo["wk0"][0]], A["early"][:, 0:eo["wk0"][0]]).then_inc(s("early_in"), 16)
            sp.dma_start(half(x, 0), tok(A["x"], 0)).then_inc(s("x_in0"), 16)
            sp.dma_start(early[:, eo["wk0"][0]:], A["early"][:, eo["wk0"][0]:]).then_inc(s("weights0_in"), 16)
            sp.dma_start(half(x, 1), tok(A["x"], 1)).then_inc(s("x_in1"), 16)
            sp.dma_start(w0[:, :, :], A["w0"]).then_inc(s("w0_in"), 16)
            sp.dma_start(lay1[:, :, :], A["attn1"]).then_inc(s("attn1_in"), 16)
            sp.dma_start(late[:, :], A["late"]).then_inc(s("late_in"), 16)
            sp.dma_start(b12f[:, :], A["b12"]).then_inc(s("b12_in"), 16)
            for i in range(2):
                sp.dma_start(w1[:, i, :], A["w1"][:, i, :]).then_inc(s(f"w1_in{i}"), 16)
            sp.wait_ge(s("w1_lo"), W1S)
            for t in range(TILES):
                if t % TS == 0:
                    sp.wait_ge(s("tile_expert"), t // TS + 1)
                e = nc.sync.value_load(texi[0:1, t:t + 1], min_val=0, max_val=X - 1)
                if t >= NW:
                    sp.wait_ge(s("y1_ps"), t - NW + 1)
                sp.dma_start(wt[:, t % NW], w1s[:, bass.ds(e, 1)]).then_inc(s(f"weights_in{t % NW}"), 16)
                if t == TS + 5:
                    sp.wait_ge(s("x4"), 1)
                    sp.dma_start(tok(out, 0), half(x, 0)).then_inc(s("stored"), 16)
            for part, (k0, k1) in enumerate(END_PARTS[1]):
                sp.wait_ge(s("x4"), 1 + part + 1)
                sp.dma_start(tok(out, 1)[:, k0:k1], x[:, K + k0:K + k1]).then_inc(s("stored"), 16)
            sp.wait_ge(s("stored"), 16 * (1 + len(END_PARTS[1])))

        @block.gpsimd
        def _(pool):
            pool.memset(nhalf[:, :], -0.5).then_inc(s("nhalf"), 1)
            pool.memset(ones_row[:, :], 1.0)
            pool.memset(ones_row32[:, :], 1.0)
            pool.memset(ones16[:, :], 1.0).then_inc(s("ones"), 1)
            pool.wait_ge(s("nhalf"), 1)
            pool.wait_ge(s("cvar"), 1)
            pool.tensor_tensor(crs[:, :], cva[:, :], nhalf[0:J, 0:1], ALU.pow).then_inc(s("crstd"), 1)

            def slot_numbers(i):
                w = S // 4
                return pool.iota(iotas[:, i * w:(i + 1) * w], [[1, w]], base=i * w, channel_multiplier=0, allow_small_or_imprecise_dtypes=True)

            def rstd(i, b):
                pool.wait_ge(s("var"), i * B + b + 1)
                pool.tensor_tensor(half(rs, b), half(va, b), half(nhalf, b), ALU.pow).then_inc(s("rstd"), 1)

            def w0_lo(i):
                pool.wait_ge(s("w0_hi"), i + 1)
                a, b = i * UW, (i + 1) * UW
                pool.tensor_tensor(w0lf[:, a:b], w0f[:, a:b], w0hf[:, a:b], ALU.subtract).then_inc(s("w0_lo"), 1)

            def w1_lo(i):
                pool.wait_ge(s("w1_hi"), i + 1)
                pool.tensor_tensor(w1_part(i, 1), w1f[:, i * F1:(i + 1) * F1], w1_part(i, 0), ALU.subtract).then_inc(s("w1_lo"), 1)

            slot_numbers(0)
            rstd(0, 0)
            slot_numbers(1)
            slot_numbers(2)
            rstd(0, 1)
            slot_numbers(3)
            pool.iota(slotc[:, :], [[P, TS]], base=0, channel_multiplier=1, allow_small_or_imprecise_dtypes=True).then_inc(s("iotas"), 1)
            for i in range(W0S):
                w0_lo(i)
            rstd(1, 0)
            for i in range(0, 6):
                w1_lo(i)

            def collect(u):
                b = u // X
                pool.wait_ge(s("y_gated_act" if gated_on_act(u) else "y_gated_dve"), gated_count(u))
                if u:
                    pool.wait_ge(s("x2"), u)
                pool.tensor_tensor(half(x, b), half(x, b), yg[:, u % 3, :].rearrange("p (k d) -> p k d", k=K), ALU.add).then_inc(s("x2"), 1)

            for u in range(2 * X):
                collect(u)
                if u == 0:
                    rstd(1, 1)
                    w1_lo(6)
                if u == X:
                    rstd(2, 0)
            w1_lo(W1_EARLY)
            rstd(2, 1)
            for i in range(W1_EARLY + 1, W1S):
                w1_lo(i)
                if i == W1_EARLY + 3:
                    rstd(3, 0)

            def z_lo(b):
                pool.wait_ge(s("z_hi"), b + 1)
                pool.tensor_tensor(half(zl, b), half(z, b), half(zh, b), ALU.subtract).then_inc(s("z_lo"), 1)

            def onehots(b):
                pool.wait_ge(s("pos"), b + 1)
                for g in range(b * NG, (b + 1) * NG):
                    for k in range(K):
                        if on_pool(g, k):
                            gather_onehot(pool, g, k).then_inc(s("onehot_pool"), 1)

            z_lo(0)
            pool.wait_ge(s("w1_lo"), W1S)
            onehots(0)
            rstd(3, 1)
            z_lo(1)
            onehots(1)

        @block.scalar
        def _(act):
            a = nc.scalar
            act.wait_ge(s("early_in"), 16)
            a.activation(tg[:, :], E("gates"), ACT.Tanh).then_inc(s("tanh"), 1)

            def zT_hi(i, b):
                act.wait_ge(s("zT_ps"), i * B + b + 1)
                a.copy(zTh[:, b, :], bank[b][:, :]).then_inc(s("zT_hi"), 1)

            def w0_hi(i):
                if i == 0:
                    act.wait_ge(s("w0_in"), 16)
                a.copy(w0hf[:, i * UW:(i + 1) * UW], w0f[:, i * UW:(i + 1) * UW]).then_inc(s("w0_hi"), 1)

            def w1_hi(i):
                if i % (W1S // 2) == 0:
                    act.wait_ge(s(f"w1_in{i // (W1S // 2)}"), 16)
                a.copy(w1_part(i, 0), w1f[:, i * F1:(i + 1) * F1]).then_inc(s("w1_hi"), 1)

            def exp0(b):
                act.wait_ge(s("shift0"), b + 1)
                a.activation(pr[:, b, 0:P], sd[:, b, 0:P], ACT.Exp, scale=SC0).then_inc(s("exp0"), 1)

            def probs0_hi(b):
                act.wait_ge(s("pT0_ps"), b + 1)
                a.copy(pTh[:, b, 0:P], bank[2 + b][:, P:2 * P]).then_inc(s("pT0_hi"), 1)

            def lexp(i, b):
                act.wait_ge(s("lshift"), i * B + b + 1)
                a.activation(half(ex, b), half(ls, b), ACT.Exp).then_inc(s("lexp"), 1)

            zT_hi(0, 0)
            act.wait_ge(s("kq0_ps"), 1)
            a.copy(kq0[:, :], bank[5][:, 0:J]).then_inc(s("kq0"), 1)
            w0_hi(0)
            act.wait_ge(s("c0_ps"), 1)
            a.copy(c0h[:, :, :, :], bank[7][0:1, 256:256 + J].rearrange("p (b j) -> p b j", b=B).unsqueeze(2).to_broadcast([1, B, 4, NC])).then_inc(s("c0_hi"), 1)
            act.wait_ge(s("mask_gated"), 1)
            act.wait_ge(s("vo0_ps"), 1)
            for k in range(K):
                last = a.activation(vo0h[:, :, k, :], bank[6][:, 0:B * D].rearrange("p (b d) -> p b d", b=B), ACT.Copy, scale=mask4g[:, k:k + 1])
            last.then_inc(s("vo0_hi"), 1)
            exp0(0)
            w0_hi(1)
            zT_hi(0, 1)
            probs0_hi(0)
            w0_hi(2)
            w0_hi(3)
            act.wait_ge(s("kv1_ps"), 1)
            for hd in range(2):
                a.activation(kb1[:, :, hd, :], bank[4][:, 0:256].rearrange("p (c j) -> p c j", c=C1), ACT.Copy, scale=E("mask2")[:, hd:hd + 1])
            for hd in range(2):
                last = a.activation(vb1[:, :, :, hd, :], bank[4][:, 256:512].rearrange("p (c b j) -> p c b j", c=C1, b=B), ACT.Copy, scale=E("mask2")[:, hd:hd + 1])
            last.then_inc(s("kv1"), 1)
            exp0(1)
            w1_hi(0)
            zT_hi(1, 0)
            probs0_hi(1)
            act.wait_ge(s("kq1_ps"), 1)
            a.copy(kq1h[:, :, :].rearrange("p b (h j) -> p h b j", h=H1), bank[5][:, :].rearrange("p (h b j) -> p h b j", h=H1, b=B)).then_inc(s("kq1_hi"), 1)
            w1_hi(1)
            w1_hi(2)
            w1_hi(3)
            lexp(0, 0)

            def hidden0(u):
                act.wait_ge(s("h_ps"), u + 1)
                if u >= 3:
                    act.wait_ge(s("y_ps"), u - 2)
                a.activation(hh[:, u % 3, :], h0_bank[u % 3][:, :], ACT.Relu).then_inc(s("h_hi"), 1)

            def gated(u):
                e, b = u % X, u // X
                act.wait_ge(s("y_ps"), u + 1)
                if u >= 3:
                    act.wait_ge(s("x2"), u - 2)
                act.wait_ge(s("gates_made"), b + 1)
                for k in range(K):
                    last = a.activation(yg[:, u % 3, k * D:(k + 1) * D], y0_bank[u % 3][:, k * D:(k + 1) * D], ACT.Copy, scale=gt[:, b * K + k, e:e + 1])
                last.then_inc(s("y_gated_act"), 1)

            def exp1(q):
                act.wait_ge(s("shift1"), q + 1)
                a.activation(pr[:, q % 2, :], sd[:, q % 2, :], ACT.Exp, scale=SC1).then_inc(s("exp1"), 1)

            def probs1_hi(q):
                act.wait_ge(s("pT1_ps"), q + 1)
                if q >= 2:
                    act.wait_ge(s("o1_ps"), q - 1)
                a.copy(pTh[:, q % 2, :], probs_bank[q][:, :]).then_inc(s("pT1_hi"), 1)

            def z_hi(b):
                a.copy(half(zh, b), half(z, b)).then_inc(s("z_hi"), 1)

            hidden0(0)
            w1_hi(4)
            hidden0(1)
            act.wait_ge(s("vo1_ps"), 1)
            a.activation(vo1h[:, :, :, :].rearrange("p b g d -> p (b g d)"), bank[7][:, :], ACT.Copy, scale=tg[:, 1:2]).then_inc(s("vo1_hi"), 1)
            w1_hi(5)
            for u in range(2 * X):
                if u + 2 < 2 * X:
                    hidden0(u + 2)
                if gated_on_act(u):
                    gated(u)
                if u == 3:
                    zT_hi(1, 1)
                if u == 6:
                    lexp(0, 1)
                if u in (1, 4, 5, 9):
                    w1_hi(6 + (1, 4, 5, 9).index(u))
                if u == X + 3:
                    zT_hi(2, 0)
                if u == X + 5:
                    exp1(0)
            w1_hi(10)
            probs1_hi(0)
            exp1(1)
            w1_hi(11)
            w1_hi(12)
            probs1_hi(1)
            zT_hi(2, 1)
            w1_hi(13)
            exp1(2)
            w1_hi(14)
            w1_hi(15)
            zT_hi(3, 0)
            probs1_hi(2)
            z_hi(0)
            lexp(1, 0)

            def sorted_hi(g):
                a0, b0 = slots(g)
                act.wait_ge(s("gather_ps"), g + 1)
                if g >= 2:
                    act.wait_ge(s("h1_ps"), group_end(g - 2))
                a.copy(zsh[:, g % 2, 0:b0 - a0], bank[gather_bank(g)][:, 0:b0 - a0]).then_inc(s("sorted_hi"), 1)

            def pos_row(b):
                act.wait_ge(s("pos_ps"), b + 1)
                a.copy(posr[:, b * N:(b + 1) * N], bank[b][:, :]).then_inc(s("pos_row"), 1)

            def y1_hi(t):
                act.wait_ge(s("y1_ps"), t + 1)
                if t >= 2:
                    act.wait_ge(s("returned"), t - 1)
                a.copy(yhl[:, t % 2, 0, :], bank[y1_bank(t)][:, 0:D]).then_inc(s("y1_hi"), 1)

            def returned_T(b):
                act.wait_ge(s("returned"), (b + 1) * TS)
                for k0, k1 in END_PARTS[b]:
                    a.copy(yT[:, k0 * P:k1 * P], bank[b][:, k0 * P:k1 * P]).then_inc(s("yT"), 1)

            sorted_hi(0)
            sorted_hi(1)
            pos_row(0)
            for t in range(TILES):
                act.wait_ge(s("h1_ps"), t + 1)
                if t >= 2:
                    act.wait_ge(s("y1_ps"), t - 1)
                a.activation(hh[:, t % 2, :], h1_bank[t % 2][:, :], ACT.Relu).then_inc(s("h1_hi"), 1)
                if t in SORTED:
                    sorted_hi(SORTED[t])
                if t:
                    y1_hi(t - 1)
                if t == 0:
                    exp1(3)
                if t == 2:
                    probs1_hi(3)
                if t == 5:
                    zT_hi(3, 1)
                    z_hi(1)
                if t == 7:
                    lexp(1, 1)
                if t == 10:
                    pos_row(1)
                if t == TS + 1:
                    returned_T(0)
            y1_hi(TILES - 1)
            returned_T(1)

        @block.tensor
        def _(pe):
            mm, tr = nc.tensor.matmul, nc.tensor.transpose

            def mm3(out_ap, sh, sl, mh, ml, start=True, stop=True):
                mm(out_ap, sh, mh, start=start, stop=False, skip_group_check=True)
                mm(out_ap, sh, ml, start=False, stop=False, skip_group_check=True)
                return mm(out_ap, sl, mh, start=False, stop=stop, skip_group_check=True)

            pe.wait_ge(s("early_in"), 16)
            pe.wait_ge(s("cz"), 1)
            tr(bank[6][0:DC, 0:J], cz[:, :], ident[0:J, 0:J]).then_inc(s("ctx_tr"), 1)
            pe.wait_ge(s("ctx_T"), 1)
            pe.wait_ge(s("weights0_in"), 16)
            mm(bank[7][:, 0:J], E("wk0", DC), c2T[:, :], start=True, stop=True)
            mm(bank[7][:, J:2 * J], E("wv0", DC), c2T[:, :], start=True, stop=True).then_inc(s("kv0_ps"), 1)

            def transpose_z(i, b):
                pe.wait_ge(s("z"), i * B + b + 1)
                for k in range(K):
                    last = tr(bank[b][:, k * P:(k + 1) * P], z[:, b * K + k, :], ident[:, :])
                last.then_inc(s("zT_ps"), 1)

            def scores0(b):
                pe.wait_ge(s("zT_lo"), b + 1)
                pe.wait_ge(s("kq0_lo"), 1)
                for k in range(K):
                    mm3(bank[2 + b][:, k * NC:(k + 1) * NC], zTh[:, b, k * P:(k + 1) * P], zTl[:, b, k * P:(k + 1) * P],
                        kq0h[:, b * NC:(b + 1) * NC], kq0l[:, b * NC:(b + 1) * NC], start=k == 0, stop=False)
                pe.wait_ge(s("c0_lo"), 1)
                mm(bank[2 + b][:, 0:P], ones_row[:, :], c0h[0:1, b], start=False, stop=False, skip_group_check=True)
                mm(bank[2 + b][:, 0:P], ones_row[:, :], c0l[0:1, b], start=False, stop=True, skip_group_check=True).then_inc(s("s0_ps"), 1)

            transpose_z(0, 0)
            pe.wait_ge(s("kv0"), 1)
            mm(bank[5][:, 0:J], E("wq0T"), kT0[:, :], start=True, stop=True).then_inc(s("kq0_ps"), 1)

            def values0(b):
                mm(bank[6][:, b * D:(b + 1) * D], vT0[:, b], E("wo0"), start=True, stop=False, skip_group_check=True)
                return mm(bank[6][:, b * D:(b + 1) * D], ones_row32[:, :], E("bo0", 1), start=False, stop=True, skip_group_check=True)

            pe.wait_ge(s("ones"), 1)
            values0(0)
            pe.wait_ge(s("kq0"), 1)
            vec = E("vecs")
            mm(bank[7][0:1, 256:256 + J], vec[:, 1:2], kq0[:, :], start=True, stop=False)
            mm(bank[7][0:1, 256:256 + J], vec[:, 2:3], kT0[:, :], start=False, stop=True).then_inc(s("c0_ps"), 1)
            values0(1).then_inc(s("vo0_ps"), 1)
            scores0(0)
            transpose_z(0, 1)
            pe.wait_ge(s("attn1_in"), 16)

            def context1(which):
                for c in range(C1):
                    last = mm(bank[4][:, which * 256 + c * J:which * 256 + (c + 1) * J], lay1[0:DC, 1 + which, c * P:(c + 1) * P], E("ctxT", DC), start=True, stop=True)
                return last

            def turn0(b):
                pe.wait_ge(s("p0"), b + 1)
                tr(bank[2 + b][:, P:2 * P], pr[:, b, 0:P], ident[:, :]).then_inc(s("pT0_ps"), 1)

            def mix0(b):
                pe.wait_ge(s("pT0_lo"), b + 1)
                mm3(bank[b][:, :], pTh[:, b, 0:P], pTl[:, b, 0:P], vo0h[:, b], vo0l[:, b]).then_inc(s("o0_ps"), 1)

            turn0(0)
            context1(0)
            pe.wait_ge(s("vo0_lo"), 1)
            mix0(0)
            context1(1).then_inc(s("kv1_ps"), 1)
            scores0(1)
            pe.wait_ge(s("kv1"), 1)

            def keys1(chunks):
                for c in chunks:
                    last = mm(bank[5][:, c * P:(c + 1) * P], lay1[:, 0, c * P:(c + 1) * P], kb1[:, c], start=True, stop=True)
                return last

            keys1(range(0, 2))

            def values1(b):
                for c in range(C1):
                    r = 64 * (c % 2)
                    at = (b * 2 + c // 2) * D
                    last = mm(bank[7][r:r + 64, at:at + D], vb1[:, c, b], lay1[:, 3, c * P:(c + 1) * P], start=True, stop=c > 0, skip_group_check=True)
                    if c == 0:
                        mm(bank[7][0:NC, at:at + D], ones_row32[:, 0:NC], E("bo1", 1), start=False, stop=True, skip_group_check=True)
                return last

            def logits(i, b):
                pe.wait_ge(s("zT_lo"), i * B + b + 1)
                pe.wait_ge(s("router"), 1)
                for k in range(K):
                    at = k * X
                    last = mm3(logit_bank[i, b][:, at:at + X], zTh[:, b, k * P:(k + 1) * P], zTl[:, b, k * P:(k + 1) * P],
                               rth[:, i // 2 * X:(i // 2 + 1) * X], rtl[:, i // 2 * X:(i // 2 + 1) * X])
                last.then_inc(s("lg_ps"), 1)

            transpose_z(1, 0)
            turn0(1)
            keys1(range(2, C1)).then_inc(s("kq1_ps"), 1)
            values1(0)
            logits(1, 0)
            pe.wait_ge(s("w0_lo"), W0S)

            def up0(u):
                e, b = u % X, u // X
                if u >= 3:
                    pe.wait_ge(s("h_lo"), u - 2)
                mm3(h0_bank[u % 3][:, :], w0h[:, 0, e * P:(e + 1) * P], w0l[:, 0, e * P:(e + 1) * P], zTh[:, b, :], zTl[:, b, :]).then_inc(s("h_ps"), 1)

            def y_taken(u):
                pe.wait_ge(s("y_gated_act" if gated_on_act(u) else "y_gated_dve"), gated_count(u))

            def down0(u):
                e, b = u % X, u // X
                pe.wait_ge(s("h_lo"), u + 1)
                if u >= 3:
                    y_taken(u - 3)
                if u == 2:
                    pe.wait_ge(s("vo1_lo"), 1)
                if u == 1:
                    pe.wait_ge(s("kq1_lo"), 1)
                for k in range(K):
                    last = mm3(y0_bank[u % 3][:, k * D:(k + 1) * D], hh[:, u % 3, k * P:(k + 1) * P], hl[:, u % 3, k * P:(k + 1) * P],
                               w0h[:, 1, e * P:(e + 1) * P], w0l[:, 1, e * P:(e + 1) * P])
                last.then_inc(s("y_ps"), 1)

            def scores1(q):
                b = q // 2
                if q == 3:
                    pe.wait_ge(s("x3"), 2)
                pe.wait_ge(s("zT_lo"), 2 * B + b + 1)
                for v in range(2):
                    k = (q % 2) * 2 + v
                    last = mm3(score_bank[q][:, v * 256:(v + 1) * 256], zTh[:, b, k * P:(k + 1) * P], zTl[:, b, k * P:(k + 1) * P], kq1h[:, b], kq1l[:, b])
                last.then_inc(s("s1_ps"), 1)

            def turn1(q):
                pe.wait_ge(s("p1"), q + 1)
                if q == 1:
                    pe.wait_ge(s("pT1_lo"), 1)
                for v in range(4):
                    last = tr(probs_bank[q][:, v * P:(v + 1) * P], pr[:, q % 2, v * P:(v + 1) * P], ident[:, :])
                last.then_inc(s("pT1_ps"), 1)

            def mix1(q):
                b = q // 2
                pe.wait_ge(s("pT1_lo"), q + 1)
                for v in range(2):
                    for g in range(2):
                        c = (v * 2 + g) * P
                        last = mm3(out1_ps(q)[:, v * D:(v + 1) * D], pTh[:, q % 2, c:c + P], pTl[:, q % 2, c:c + P],
                                   vo1h[:, b, g, :], vo1l[:, b, g, :], start=g == 0, stop=g == 1)
                last.then_inc(s("o1_ps"), 1)

            up0(0)
            mix0(1)
            up0(1)
            values1(1).then_inc(s("vo1_ps"), 1)
            for u in range(2 * X):
                if u + 2 < 2 * X:
                    up0(u + 2)
                if u == X + 5:
                    scores1(0)
                down0(u)
                if u == 3:
                    transpose_z(1, 1)
                if u == 5:
                    logits(1, 1)
                if u == X + 3:
                    transpose_z(2, 0)
            scores1(1)
            y_taken(2 * X - 3)
            y_taken(2 * X - 2)
            y_taken(2 * X - 1)
            turn1(0)
            mix1(0)
            turn1(1)
            transpose_z(2, 1)
            mix1(1)
            scores1(2)
            scores1(3)
            transpose_z(3, 0)
            turn1(2)
            logits(3, 0)

            def ranks(b):
                pe.wait_ge(s("chosen"), b + 1)
                mm(rank_ps(b)[:, 0:K * X], before16[:, :], half(oh16, b), start=True, stop=True, skip_group_check=True)
                for k in range(K):
                    last = mm(rank_ps(b)[:, (k + 1) * X:].rearrange("p (t e) -> p t e", e=X), ones16[:, :],
                              oh16[:, b * K + k, :].unsqueeze(1).to_broadcast([P, K - k, X]), start=False, stop=True, skip_group_check=True)
                last.then_inc(s("rank_ps"), 1)

            def pos_rows(b):
                pe.wait_ge(s("diag"), b + 1)
                for k in range(K):
                    last = mm(bank[b][:, k * P:(k + 1) * P], ones16[:, :], diag[:, b * K + k, :], start=True, stop=True)
                last.then_inc(s("pos_ps"), 1)

            def gather(g, k0, k1):
                a0, b0 = slots(g)
                w = b0 - a0
                pe.wait_ge(s("z_lo"), g // NG + 1)
                if last_user(gather_bank, g) is not None and k0 == 0:
                    pe.wait_ge(s("sorted_lo"), last_user(gather_bank, g) + 1)
                for k in range(k0, k1):
                    if on_pool(g, k):
                        pe.wait_ge(s("onehot_pool"), onehots_made(True, g, k))
                    else:
                        pe.wait_ge(s("onehot"), onehots_made(False, g, k))
                    t = g // NG * K + k
                    mm(bank[gather_bank(g)][:, 0:w], zh[:, t, :], G[:, t, a0:b0], start=k == 0, stop=False)
                    last = mm(bank[gather_bank(g)][:, 0:w], zl[:, t, :], G[:, t, a0:b0], start=False, stop=k == K - 1)
                if k1 == K:
                    last.then_inc(s("gather_ps"), 1)

            def up1(t):
                g = group_of[t]
                o = (t % TS - GROUPS[g % NG][0]) * P
                if t % TS == 0:
                    pe.wait_ge(s("tile_select"), t // TS + 1)
                if t == 1:
                    pe.wait_ge(s("x3"), 3)
                pe.wait_ge(s(f"weights_in{t % NW}"), 16 * (t // NW + 1))
                if t % TS == GROUPS[g % NG][0]:
                    pe.wait_ge(s("sorted_lo"), g + 1)
                for c in range(M1):
                    wh, wl = (wt[:, t % NW, 0, part, c * P:(c + 1) * P] for part in range(2))
                    mm3(h1_bank[t % 2][:, c * P:(c + 1) * P], wh, wl, zsh[:, g % 2, o:o + P], zsl[:, g % 2, o:o + P], stop=False)
                    last = mm(h1_bank[t % 2][:, c * P:(c + 1) * P], b12s[:, c * P:(c + 1) * P], sel[:, t // TS, t % TS:t % TS + 1].to_broadcast([BR, P]),
                              start=False, stop=True, skip_group_check=True)
                last.then_inc(s("h1_ps"), 1)

            def down1(t):
                pe.wait_ge(s("h1_lo"), t + 1)
                if last_user(y1_bank, t) is not None:
                    pe.wait_ge(s("y1_lo"), last_user(y1_bank, t) + 1)
                for c in range(M1):
                    wh, wl = (wt[:, t % NW, 1, part, c * P:(c + 1) * P] for part in range(2))
                    hc, lc = (h[:, t % 2, c * P:(c + 1) * P] for h in (hh, hl))
                    mm(bank[y1_bank(t)][:, 0:D], hc, wh, start=c == 0, stop=False, skip_group_check=True)
                    mm(bank[y1_bank(t)][:, 0:D], lc, wh, start=False, stop=False, skip_group_check=True)
                    mm(bank[y1_bank(t)][:, 0:D], hc, wl, start=False, stop=False, skip_group_check=True)
                mm(bank[y1_bank(t)][:, 0:D], sel[:, t // TS, t % TS:t % TS + 1].to_broadcast([BR, P]), b12s[:, F1:F1 + D],
                   start=False, stop=True, skip_group_check=True).then_inc(s("y1_ps"), 1)

            def give_back(t):
                b = t // TS
                if t % TS == 0:
                    pe.wait_ge(s("pos_row"), b + 1)
                pe.wait_ge(s("return_onehot"), t + 1)
                pe.wait_ge(s("y1_hi"), t + 1)
                mm(bank[b][:, :], yhl[:, t % 2, 0, :], Q[:, t % 2, :], start=t % TS == 0, stop=False, skip_group_check=True)
                pe.wait_ge(s("y1_lo"), t + 1)
                mm(bank[b][:, :], yhl[:, t % 2, 1, :], Q[:, t % 2, :], start=False, stop=t % TS == TS - 1,
                   skip_group_check=True).then_inc(s("returned"), 1)

            def turn_back(b):
                for part, (k0, k1) in enumerate(END_PARTS[b]):
                    pe.wait_ge(s("yT"), b + part + 1)
                    for k in range(k0, k1):
                        last = tr(turned_bank[b][part][:, k * D:(k + 1) * D], yT[:, k * P:(k + 1) * P], ident[:, :])
                    last.then_inc(s("turned"), 1)

            mix1(2)
            ranks(0)
            gather(0, 0, K)
            gather(1, 0, K)
            pos_rows(0)
            up1(0)
            for t in range(TILES):
                if t + 1 < TILES:
                    up1(t + 1)
                if t in GATHER:
                    gather(*GATHER[t])
                down1(t)
                if t:
                    give_back(t - 1)
                if t == 0:
                    turn1(3)
                if t == 2:
                    mix1(3)
                if t == 4:
                    transpose_z(3, 1)
                if t == 5:
                    logits(3, 1)
                if t == 6:
                    ranks(1)
                if t == 9:
                    pos_rows(1)
                if t == TS + 1:
                    turn_back(0)
            give_back(TILES - 1)
            turn_back(1)

        @block.vector
        def _(dve):
            v = nc.vector
            step = [0]

            def link(ins):
                step[0] += 1
                ins.then_inc(s("dve_step"), 1)
                dve.wait_ge(s("dve_step"), step[0])

            def stats(i, b):
                for k in range(K):
                    last = v.bn_stats(st[:, b * K + k, :], x[:, b * K + k, :])
                link(last)
                for k in range(K):
                    last = v.bn_aggr(mv[:, b * K + k, :], st[:, b * K + k, :])
                link(last)
                if i == 0:
                    v.tensor_scalar(half(va, b), mv[:, b * K:(b + 1) * K, 1], 1.0 + EPS, EPS * EPS, ALU.mult, ALU.add).then_inc(s("var"), 1)
                else:
                    v.tensor_scalar(half(va, b), mv[:, b * K:(b + 1) * K, 1], EPS, None, ALU.add).then_inc(s("var"), 1)

            def apply(i, b):
                dve.wait_ge(s("rstd"), i * B + b + 1)
                for k in range(K):
                    t = b * K + k
                    last = v.tensor_scalar(z[:, t, :], x[:, t, :], mv[:, t, 0:1], rs[:, t:t + 1], ALU.subtract, ALU.mult)
                last.then_inc(s("z"), 1)

            def zT_lo(i, b):
                dve.wait_ge(s("zT_hi"), i * B + b + 1)
                v.tensor_tensor(zTl[:, b, :], bank[b][:, :], zTh[:, b, :], ALU.subtract).then_inc(s("zT_lo"), 1)

            def split(hi, lo, src):
                link(v.tensor_copy(hi, src))
                return v.tensor_tensor(lo, src, hi, ALU.subtract)

            dve.wait_ge(s("early_in"), 16)
            link(v.bn_stats(cst[:, :], E("ctx", J)))
            link(v.bn_aggr(cmv[:, :], cst[:, :]))
            v.tensor_scalar(cva[:, :], cmv[:, 1:2], EPS, None, ALU.add).then_inc(s("cvar"), 1)
            dve.wait_ge(s("crstd"), 1)
            v.tensor_scalar(cz[:, :], E("ctx", J), cmv[:, 0:1], crs[:, 0:1], ALU.subtract, ALU.mult).then_inc(s("cz"), 1)
            dve.wait_ge(s("x_in0"), 16)
            stats(0, 0)
            vec = E("vecs")
            dve.wait_ge(s("ctx_tr"), 1)
            v.tensor_scalar(c2T[:, :], bank[6][0:DC, 0:J], vec[0:DC, 5:6], vec[0:DC, 6:7], ALU.mult, ALU.add).then_inc(s("ctx_T"), 1)
            dve.wait_ge(s("tanh"), 1)
            v.tensor_scalar(mask4g[:, :], E("mask4"), tg[:, 0:1], None, ALU.mult).then_inc(s("mask_gated"), 1)
            apply(0, 0)
            dve.wait_ge(s("kv0_ps"), 1)
            v.tensor_scalar(kT0[:, :], bank[7][:, 0:J], vec[:, 3:4], None, ALU.add)
            v.tensor_scalar(vT0[:, :, :, :], bank[7][:, J:2 * J].rearrange("p (b j) -> p b j", b=B).unsqueeze(2).to_broadcast([P, B, 4, NC]),
                            vec[:, 4:5], None, ALU.add).then_inc(s("kv0"), 1)
            dve.wait_ge(s("x_in1"), 16)
            stats(0, 1)
            dve.wait_ge(s("kq0_ps"), 1)
            dve.wait_ge(s("kq0"), 1)
            link(v.tensor_scalar(kq0h[:, :], bank[5][:, 0:J], vec[:, 0:1], None, ALU.mult))
            v.scalar_tensor_tensor(kq0l[:, :], bank[5][:, 0:J], vec[:, 0:1], kq0h[:, :], ALU.mult, ALU.subtract).then_inc(s("kq0_lo"), 1)
            zT_lo(0, 0)
            dve.wait_ge(s("c0_hi"), 1)
            v.tensor_tensor(c0l[:, :, :, :], bank[7][0:1, 256:256 + J].rearrange("p (b j) -> p b j", b=B).unsqueeze(2).to_broadcast([1, B, 4, NC]),
                            c0h[:, :, :, :], ALU.subtract).then_inc(s("c0_lo"), 1)
            apply(0, 1)

            def softmax_shift(Sc, q, Gr, w, shift):
                sq = sd[:, q, 0:Gr * w].rearrange("p (g w) -> p g w", g=Gr)
                link(v.tensor_reduce(mx[:, q, 0:Gr], Sc, AX.X, ALU.max))
                v.tensor_tensor(sq, Sc, bc(mx[:, q, 0:Gr], [P, Gr, w]), ALU.subtract).then_inc(s(shift), 1)

            def softmax_divide(q, Gr, w, expd, made, count):
                pq = pr[:, q, 0:Gr * w].rearrange("p (g w) -> p g w", g=Gr)
                dve.wait_ge(s(expd), count)
                link(v.tensor_reduce(sm[:, q, 0:Gr], pq, AX.X, ALU.add))
                link(v.reciprocal(ri[:, q, 0:Gr], sm[:, q, 0:Gr]))
                v.tensor_tensor(pq, pq, bc(ri[:, q, 0:Gr], [P, Gr, w]), ALU.mult).then_inc(s(made), 1)

            def shift0(b):
                dve.wait_ge(s("s0_ps"), b + 1)
                softmax_shift(bank[2 + b][:, 0:P].rearrange("p (k j) -> p k j", k=K), b, K, NC, "shift0")

            def probs0_lo(b):
                dve.wait_ge(s("pT0_hi"), b + 1)
                v.tensor_tensor(pTl[:, b, 0:P], bank[2 + b][:, P:2 * P], pTh[:, b, 0:P], ALU.subtract).then_inc(s("pT0_lo"), 1)

            def first_out(b):
                dve.wait_ge(s("o0_ps"), b + 1)
                link(v.tensor_tensor(half(x, b), bank[b][:, :].rearrange("p (k d) -> p k d", k=K), half(x, b), ALU.add))

            shift0(0)
            softmax_divide(0, K, NC, "exp0", "p0", 1)
            dve.wait_ge(s("vo0_hi"), 1)
            for k in range(K):
                last = v.scalar_tensor_tensor(vo0l[:, :, k, :], bank[6][:, 0:B * D].rearrange("p (b d) -> p b d", b=B), mask4g[:, k:k + 1],
                                              vo0h[:, :, k, :], ALU.mult, ALU.subtract)
            last.then_inc(s("vo0_lo"), 1)
            probs0_lo(0)
            zT_lo(0, 1)
            dve.wait_ge(s("late_in"), 16)
            split(rth[:, :], rtl[:, :], late[:, 0:2 * X]).then_inc(s("router"), 1)
            v.tensor_copy(before16[:, :], Lt("before"))
            v.tensor_copy(ident16[:, :], ident)
            first_out(0)
            stats(1, 0)
            shift0(1)
            apply(1, 0)
            softmax_divide(1, K, NC, "exp0", "p0", 2)
            dve.wait_ge(s("b12_in"), 16)
            link(v.tensor_copy(b12s[:, :], b12f[:, :]))
            v.tensor_tensor(b12s[32:BR, :], b12f[32:BR, :], b12s[32:BR, :], ALU.subtract)
            zT_lo(1, 0)
            probs0_lo(1)

            def gate(i, b):
                full = [P, K, X]
                dve.wait_ge(s("lg_ps"), i * B + b + 1)
                ps = logit_bank[2 * i + 1, b][:, 0:K * X].rearrange("p (t e) -> p t e", t=K)
                if i == 0:
                    link(v.tensor_copy(half(lg, b), ps))
                else:
                    link(v.tensor_tensor(half(lg, b), ps, Lt("b_gate").unsqueeze(1).to_broadcast(full), ALU.add))
                for k in range(K):
                    last = v.max(m8[:, b * K + k, :], lg[:, b * K + k, :])
                link(last)

                def shift():
                    v.tensor_tensor(half(ls, b), half(lg, b), bc(m8[:, b * K:(b + 1) * K, 0], full), ALU.subtract).then_inc(s("lshift"), 1)

                if i == 0:
                    shift()
                for k in range(K):
                    last = v.max_index(i8[:, b * K + k, :], m8[:, b * K + k, :], lg[:, b * K + k, :])
                link(last)
                which = Lt("iota8").unsqueeze(1).to_broadcast(full)
                if i == 1:
                    v.tensor_tensor(half(oh16, b), which, bc(i8[:, b * K:(b + 1) * K, 0], full), ALU.is_equal).then_inc(s("chosen"), 1)
                    shift()
                v.tensor_tensor(half(oh, b), which, bc(i8[:, b * K:(b + 1) * K, 0], full), ALU.is_equal)
                if i == 0:
                    link(v.tensor_tensor(half(oh2, b), which, bc(i8[:, b * K:(b + 1) * K, 1], full), ALU.is_equal))
                    link(v.tensor_tensor(half(oh, b), half(oh, b), half(oh2, b), ALU.add))

            def gate_values(i, b):
                full = [P, K, X]
                dve.wait_ge(s("lexp"), i * B + b + 1)
                link(v.tensor_reduce(half(zs, b), half(ex, b), AX.X, ALU.add))
                link(v.reciprocal(half(zs, b), half(zs, b)))
                link(v.tensor_scalar(half(zs, b), half(zs, b), tg[:, 2 + i:3 + i], None, ALU.mult))
                if i == 0:
                    link(v.tensor_tensor(half(gt, b), half(ex, b), half(oh, b), ALU.mult))
                    v.tensor_tensor(half(gt, b), half(gt, b), bc(half(zs, b), full), ALU.mult).then_inc(s("gates_made"), 1)

            gate(0, 0)

            def lo0(u):
                dve.wait_ge(s("h_hi"), u + 1)
                v.scalar_tensor_tensor(hl[:, u % 3, :], h0_bank[u % 3][:, :], 0.0, hh[:, u % 3, :], ALU.max, ALU.subtract).then_inc(s("h_lo"), 1)

            def gated(u):
                e, b = u % X, u // X
                dve.wait_ge(s("y_ps"), u + 1)
                dve.wait_ge(s("gates_made"), b + 1)
                if u >= 3:
                    dve.wait_ge(s("x2"), u - 2)
                v.tensor_tensor(yg[:, u % 3, :].rearrange("p (k d) -> p k d", k=K), y0_bank[u % 3][:, :].rearrange("p (k d) -> p k d", k=K),
                                bc(gt[:, b * K:(b + 1) * K, e], [P, K, D]), ALU.mult).then_inc(s("y_gated_dve"), 1)

            def shift1(q):
                dve.wait_ge(s("s1_ps"), q + 1)
                if q >= 2:
                    dve.wait_ge(s("exp1"), q - 1)
                softmax_shift(score_bank[q][:, :].rearrange("p (g j) -> p g j", j=NC), q % 2, 16, NC, "shift1")

            def divide1(q):
                softmax_divide(q % 2, 16, NC, "exp1", "p1", q + 1)

            def probs1_lo(q):
                dve.wait_ge(s("pT1_hi"), q + 1)
                v.tensor_tensor(pTl[:, q % 2, :], probs_bank[q][:, :], pTh[:, q % 2, :], ALU.subtract).then_inc(s("pT1_lo"), 1)

            def out1(q):
                dve.wait_ge(s("o1_ps"), q + 1)
                v.tensor_tensor(x[:, 2 * q:2 * q + 2, :], out1_ps(q).rearrange("p (u d) -> p u d", u=2),
                                x[:, 2 * q:2 * q + 2, :], ALU.add).then_inc(s("x3"), 1)

            lo0(0)
            dve.wait_ge(s("kq1_hi"), 1)
            v.tensor_tensor(kq1l[:, :, :].rearrange("p b (h j) -> p h b j", h=H1), bank[5][:, :].rearrange("p (h b j) -> p h b j", h=H1, b=B),
                            kq1h[:, :, :].rearrange("p b (h j) -> p h b j", h=H1), ALU.subtract).then_inc(s("kq1_lo"), 1)
            gate_values(0, 0)
            lo0(1)
            dve.wait_ge(s("vo1_hi"), 1)
            v.scalar_tensor_tensor(vo1l[:, :, :, :].rearrange("p b g d -> p (b g d)"), bank[7][:, :], tg[:, 1:2],
                                   vo1h[:, :, :, :].rearrange("p b g d -> p (b g d)"), ALU.mult, ALU.subtract).then_inc(s("vo1_lo"), 1)
            for u in range(2 * X):
                if u + 2 < 2 * X:
                    lo0(u + 2)
                if not gated_on_act(u):
                    gated(u)
                if u == 0:
                    first_out(1)
                    stats(1, 1)
                if u == 2:
                    apply(1, 1)
                if u == 4:
                    zT_lo(1, 1)
                if u == 6:
                    gate(0, 1)
                if u == 7:
                    gate_values(0, 1)
                if u == X:
                    dve.wait_ge(s("x2"), X)
                    stats(2, 0)
                if u == X + 1:
                    apply(2, 0)
                if u == X + 3:
                    zT_lo(2, 0)
                if u == X + 5:
                    shift1(0)
            divide1(0)
            shift1(1)
            probs1_lo(0)
            dve.wait_ge(s("x2"), 2 * X)
            stats(2, 1)
            divide1(1)
            apply(2, 1)
            out1(0)
            probs1_lo(1)
            zT_lo(2, 1)
            out1(1)
            dve.wait_ge(s("x3"), 2)
            stats(3, 0)
            shift1(2)
            apply(3, 0)
            divide1(2)
            zT_lo(3, 0)
            probs1_lo(2)
            gate(1, 0)

            def bases(b):
                dve.wait_ge(s("rank_ps"), b + 1)
                rank = rank_ps(b).rearrange("p (t e) -> p t e", e=X)
                link(v.tensor_tensor(cmp[:, :, :], bc(rank[:, K, :], [P, X, 8]), Lt("thresholds").rearrange("p (e j) -> p e j", e=X), ALU.is_gt))
                link(v.tensor_reduce(ntile[:, b], cmp[:, :, :], AX.X, ALU.add))
                link(v.tensor_tensor(bas8[:, :, :], ntile[:, b].unsqueeze(1).to_broadcast([P, X, X]), Lt("before8").rearrange("p (e j) -> p e j", e=X), ALU.mult))
                link(v.tensor_reduce(base[:, b], bas8[:, :, :], AX.X, ALU.add))

            def positions(b):
                rank = rank_ps(b).rearrange("p (t e) -> p t e", e=X)
                v.tensor_tensor(pt8[:, :, :], rank[:, 0:K, :], base[:, b].unsqueeze(1).to_broadcast([P, K, X]), ALU.add)
                link(v.scalar_tensor_tensor(send[:, :], ntile[0:BR, b], float(P), base[0:BR, b], ALU.mult, ALU.add))
                v.tensor_tensor(pt8[:, :, :], pt8[:, :, :], half(oh, b), ALU.mult)
                link(v.tensor_tensor(tcmp[:, :, :], send[:, :].unsqueeze(1).to_broadcast([BR, TS, X]), Lt("tile_starts", BR).rearrange("p (t e) -> p t e", t=TS), ALU.is_le))
                v.tensor_reduce(tex[:, :], tcmp[:, :, :], AX.X, ALU.add).then_inc(s("tile_counts"), 1)
                v.tensor_reduce(half(pos, b), pt8[:, :, :], AX.X, ALU.add).then_inc(s("pos"), 1)
                dve.wait_ge(s("tile_counts"), b + 1)
                v.tensor_scalar(texi[:, b * TS:(b + 1) * TS], tex[0:1, :], float(X - 1), None, ALU.min).then_inc(s("tile_expert"), 1)
                v.tensor_scalar(sel[:, b], tex[:, :], Lt("row_expert", BR), None, ALU.is_equal).then_inc(s("tile_select"), 1)
                dve.wait_ge(s("pos"), b + 1)

            def onehots(g):
                for k in range(K):
                    if not on_pool(g, k):
                        gather_onehot(v, g, k).then_inc(s("onehot"), 1)

            def pos_diag(b):
                for k in range(K):
                    last = v.tensor_scalar(diag[:, b * K + k, :], ident16[:, :], pos[:, b * K + k:b * K + k + 1], None, ALU.mult)
                last.then_inc(s("diag"), 1)

            def sorted_lo(g):
                a0, b0 = slots(g)
                dve.wait_ge(s("sorted_hi"), g + 1)
                v.tensor_tensor(zsl[:, g % 2, 0:b0 - a0], bank[gather_bank(g)][:, 0:b0 - a0], zsh[:, g % 2, 0:b0 - a0], ALU.subtract).then_inc(s("sorted_lo"), 1)

            def return_onehot(t):
                b = t // TS
                if t >= 2:
                    dve.wait_ge(s("returned"), t - 1)
                v.tensor_scalar(Q[:, t % 2, :], posr[:, b * N:(b + 1) * N], slotc[:, t % TS:t % TS + 1], None, ALU.is_equal).then_inc(s("return_onehot"), 1)

            def y1_lo(t):
                dve.wait_ge(s("y1_hi"), t + 1)
                v.tensor_tensor(yhl[:, t % 2, 1, :], bank[y1_bank(t)][:, 0:D], yhl[:, t % 2, 0, :], ALU.subtract).then_inc(s("y1_lo"), 1)

            def last_out(b):
                for part, (k0, k1) in enumerate(END_PARTS[b]):
                    dve.wait_ge(s("turned"), b + part + 1)
                    for k in range(k0, k1):
                        t = b * K + k
                        last = v.scalar_tensor_tensor(x[:, t, :], turned_bank[b][part][:, k * D:(k + 1) * D], zs[:, t:t + 1], x[:, t, :], ALU.mult, ALU.add)
                    last.then_inc(s("x4"), 1)

            bases(0)
            positions(0)
            dve.wait_ge(s("iotas"), 1)
            dve.wait_ge(s("w1_lo"), W1S)
            onehots(0)
            onehots(1)
            pos_diag(0)
            sorted_lo(0)
            out1(2)
            shift1(3)
            sorted_lo(1)
            onehots(2)
            dve.wait_ge(s("pos_row"), 1)
            for t in range(TILES):
                dve.wait_ge(s("h1_hi"), t + 1)
                v.scalar_tensor_tensor(hl[:, t % 2, :], h1_bank[t % 2][:, :], 0.0, hh[:, t % 2, :], ALU.max, ALU.subtract).then_inc(s("h1_lo"), 1)
                if t in SORTED:
                    sorted_lo(SORTED[t])
                if t:
                    y1_lo(t - 1)
                return_onehot(t)
                if t == 0:
                    divide1(3)
                if t == 2:
                    probs1_lo(3)
                if t == 3:
                    out1(3)
                    dve.wait_ge(s("x3"), T // 2)
                    stats(3, 1)
                if t == 4:
                    apply(3, 1)
                if t == 5:
                    zT_lo(3, 1)
                if t == 6:
                    gate(1, 1)
                if t == 7:
                    bases(1)
                if t == 8:
                    positions(1)
                if t == 9:
                    onehots(4)
                    pos_diag(1)
                if t == 11:
                    gate_values(1, 0)
                    gate_values(1, 1)
                if t == TS - 1:
                    dve.wait_ge(s("pos_row"), 2)
                if t == TS + 2:
                    last_out(0)
            y1_lo(TILES - 1)
            last_out(1)


_OUT = ((2, 512, 128), "float32")


def kernel(**inputs):
    import numpy as np
    import concourse.bacc as bacc
    from concourse import mybir
    from concourse.bass_utils import run_bass_kernel_spmd

    a = {k: np.asarray(v) for k, v in inputs.items()}
    X = a["L1_ffn_w_gate"].shape[1]
    M = a["L1_ffn_W1"].shape[2] // P
    J, DC = a["ctx_768"].shape[0] * a["ctx_768"].shape[1], a["ctx_768"].shape[2]
    TS = a["x"].shape[1] // P + X - 1

    def table(columns, parts):
        at, width = offsets(columns)
        out = np.zeros((P, width), np.float32)
        for name, part in parts.items():
            lo, hi = at[name]
            part = np.asarray(part)
            out[0:part.shape[0], lo:hi] = part.reshape(part.shape[0], hi - lo)
        return out

    def rows(v, n=P):
        return np.broadcast_to(v.reshape(1, -1), (n, v.size))

    vecs = np.zeros((P, 7), np.float32)
    for i, name in enumerate(("ln1_g", "ln1_b", "bq", "bk", "bv", "ln2_g", "ln2_b")):
        v = a["L0_xattn_" + name]
        vecs[0:v.size, i] = v
    ctx = a["ctx_768"].reshape(J, DC)
    p = np.arange(P)
    sent = {
        "x": a["x"],
        "early": table(EARLY, {
            "ident": np.eye(P, dtype=np.float32), "ctx": ctx, "ctxT": ctx.T,
            "gates": rows(np.concatenate([a["g_xattn"], a["g_ffn"]])), "vecs": vecs,
            "mask4": p[:, None] // 32 == np.arange(4), "mask2": p[:, None] // 64 == np.arange(2),
            "wk0": a["L0_xattn_Wk"], "wv0": a["L0_xattn_Wv"], "wq0T": a["L0_xattn_Wq"].T, "wo0": a["L0_xattn_Wo"],
            "bo0": rows(a["L0_xattn_bo"], 1), "bo1": rows(a["L1_xattn_bo"], 1),
        }),
        "late": table(LATE, {
            "routerT": a["L0_ffn_router_w"].T, "w_gate": a["L1_ffn_w_gate"], "b_gate": rows(a["L1_ffn_b_gate"]),
            "before": p[:, None] < p[None, :], "iota8": rows(np.arange(X)),
            "before8": rows(P * (np.arange(X)[None, :] < np.arange(X)[:, None])),
            "thresholds": rows(np.broadcast_to(P * np.arange(8), (X, 8))),
            "tile_starts": rows(np.repeat(P * np.arange(TS), X)),
            "row_expert": np.where(p % 32 < X, p % 32, -1),
        }),
        "w0": np.stack([a["L0_ffn_w1"].transpose(1, 0, 2).reshape(P, -1), a["L0_ffn_w2"].transpose(1, 0, 2).reshape(P, -1)], 1),
        "b12": np.zeros((32 + X, 512 + P), np.float32),
        "attn1": np.zeros((P, 4, 512), np.float32),
        "w1": np.stack([a["L1_ffn_W1"].transpose(1, 0, 2).reshape(P, -1),
                        a["L1_ffn_W2"].reshape(X, M, P, P).transpose(2, 0, 1, 3).reshape(P, -1)], 1),
    }
    for r in (0, 32):
        sent["b12"][r:r + X] = np.concatenate([a["L1_ffn_b1"], a["L1_ffn_b2"]], 1)
    sent["attn1"][:, 0] = a["L1_xattn_Wq"].T.reshape(4, P, P).transpose(1, 0, 2).reshape(P, -1)
    sent["attn1"][0:DC, 1] = a["L1_xattn_Wk"]
    sent["attn1"][0:DC, 2] = a["L1_xattn_Wv"]
    sent["attn1"][:, 3] = a["L1_xattn_Wo"].reshape(4, P, P).transpose(1, 0, 2).reshape(P, -1)

    nc = bacc.Bacc("TRN2", target_bir_lowering=False, num_devices=1)
    arrays, args = {}, {}
    for name, value in sent.items():
        value = np.ascontiguousarray(value)
        arrays[f"in_{name}_dram"] = value
        args[name] = nc.dram_tensor(f"in_{name}_dram", value.shape, mybir.dt.from_np(value.dtype), kind="ExternalInput").ap()
    out = nc.dram_tensor("out_0_dram", _OUT[0], mybir.dt.from_np(np.dtype(_OUT[1])), kind="ExternalOutput").ap()
    gated_blocks_kernel(nc, args, out)
    r = run_bass_kernel_spmd(nc, [arrays], core_ids=[0])
    return r.results[0]["out_0_dram"]
```
